# Optimizing a Trainium2 kernel written in Bass

```python
import numpy as np
import jax
import jax.numpy as jnp

def _softmax(x, axis=-1):
    return jax.nn.softmax(x, axis=axis)

def _gelu(x):
    return jax.nn.gelu(x, approximate=True)

def _silu(x):
    return jax.nn.silu(x)

def _sigmoid(x):
    return jax.nn.sigmoid(x)

def _layernorm(x, axis=-1, eps=1e-05):
    m = jnp.mean(x, axis=axis, keepdims=True)
    v = jnp.var(x, axis=axis, keepdims=True)
    return (x - m) / jnp.sqrt(v + eps)

def _scatter_add(tgt, idx, src, axis=0):
    return tgt.at[idx].add(src)

def _segment_sum(src, seg, n):
    return jax.ops.segment_sum(src, seg, n)
kernel_name = 'mk_prb_d1_jaxref_r8_1f78e4'

def setup_inputs(seed: int=0):
    np.random.seed(seed)
    _w = jnp.asarray

    def _L0_attn_setup():
        import jax, jax.numpy as jnp
        import numpy as np
        B, S, HID = (2, 256, 128)
        NH = 16
        HD = HID // NH
        BASE = 10000.0

        def rotate_half(x):
            x1, x2 = jnp.split(x, 2, axis=-1)
            return jnp.concatenate((-x2, x1), axis=-1)
        key = jax.random.key(seed)
        ks = jax.random.split(key, 9)
        sc = 1.0 / np.sqrt(HID)
        inp = {'x': jax.random.normal(ks[0], (B, S, HID), dtype=jnp.float32), 'wq': jax.random.normal(ks[1], (HID, HID), dtype=jnp.float32) * sc, 'bq': jnp.zeros((HID,), dtype=jnp.float32), 'wk': jax.random.normal(ks[2], (HID, HID), dtype=jnp.float32) * sc, 'bk': jnp.zeros((HID,), dtype=jnp.float32), 'wv': jax.random.normal(ks[3], (HID, HID), dtype=jnp.float32) * sc, 'bv': jnp.zeros((HID,), dtype=jnp.float32), 'wo': jax.random.normal(ks[4], (HID, HID), dtype=jnp.float32) * sc, 'bo': jnp.zeros((HID,), dtype=jnp.float32)}
        return inp
    _L0_attn_in = _L0_attn_setup()

    def _L0_ffn_setup():
        import jax, jax.numpy as jnp
        import numpy as np
        B, S, D = (2, 256, 128)
        H, E, P, K = (8, 8, 128, 2)
        SCALE = 1.0 / np.sqrt(P)

        def _get_sel_gate(x, w, route_scale):
            logits = jnp.einsum('bsd,ed->bse', x, w).astype(jnp.float32)
            raw = logits.reshape(x.shape[0], x.shape[1], H, E)
            probs = jax.nn.sigmoid(raw)
            vals, idx = jax.lax.top_k(probs, K)
            vals = vals / jnp.clip(vals.sum(-1, keepdims=True), 1e-09)
            vals = vals * route_scale
            gate = (jax.nn.one_hot(idx, E, dtype=vals.dtype) * vals[..., None]).sum(-2)
            return gate
        key = jax.random.key(seed)
        ks = jax.random.split(key, 8)
        std = 1.0 / np.sqrt(D)
        return {'x': jax.random.normal(ks[0], (B, S, D), jnp.float32), 'q_w': jax.random.normal(ks[1], (H * P, D), jnp.float32) * std, 'k_w': jax.random.normal(ks[2], (H * P, D), jnp.float32) * std, 'v_w': jax.random.normal(ks[3], (H * E, D, P), jnp.float32) * std, 'o_w': jax.random.normal(ks[4], (H * E, P, D), jnp.float32) * (1.0 / np.sqrt(H * P)), 'sel_v_w': jax.random.normal(ks[5], (H * E, D), jnp.float32) * std, 'sel_o_w': jax.random.normal(ks[6], (H * E, D), jnp.float32) * std, 'route_scale': jnp.ones((1,), jnp.float32)}
    _L0_ffn_in = _L0_ffn_setup()
    _d = {'L0_attn_x': _L0_attn_in['x'], 'L0_attn_wq': _L0_attn_in['wq'], 'L0_attn_bq': _L0_attn_in['bq'], 'L0_attn_wk': _L0_attn_in['wk'], 'L0_attn_bk': _L0_attn_in['bk'], 'L0_attn_wv': _L0_attn_in['wv'], 'L0_attn_bv': _L0_attn_in['bv'], 'L0_attn_wo': _L0_attn_in['wo'], 'L0_attn_bo': _L0_attn_in['bo'], 'L0_ffn_q_w': _L0_ffn_in['q_w'], 'L0_ffn_k_w': _L0_ffn_in['k_w'], 'L0_ffn_v_w': _L0_ffn_in['v_w'], 'L0_ffn_o_w': _L0_ffn_in['o_w'], 'L0_ffn_sel_v_w': _L0_ffn_in['sel_v_w'], 'L0_ffn_sel_o_w': _L0_ffn_in['sel_o_w'], 'L0_ffn_route_scale': _L0_ffn_in['route_scale']}
    _x0 = _d['L0_attn_x']
    _d['L0_attn_x'] = jax.random.normal(jax.random.fold_in(jax.random.key(seed), 1), (2, 1024, 128), dtype=_x0.dtype)
    del _x0
    return _d

def reference(L0_attn_x, L0_attn_wq, L0_attn_bq, L0_attn_wk, L0_attn_bk, L0_attn_wv, L0_attn_bv, L0_attn_wo, L0_attn_bo, L0_ffn_q_w, L0_ffn_k_w, L0_ffn_v_w, L0_ffn_o_w, L0_ffn_sel_v_w, L0_ffn_sel_o_w, L0_ffn_route_scale):

    def _L0_attn_ref(x, wq, bq, wk, bk, wv, bv, wo, bo):
        import jax, jax.numpy as jnp
        import numpy as np
        B, S, HID = (2, 256, 128)
        NH = 16
        HD = HID // NH
        BASE = 10000.0

        def rotate_half(x):
            x1, x2 = jnp.split(x, 2, axis=-1)
            return jnp.concatenate((-x2, x1), axis=-1)
        b, s, _ = x.shape

        def proj(w, bias):
            return (x @ w.T + bias).reshape(b, s, NH, HD).transpose(0, 2, 1, 3)
        q = proj(wq, bq)
        k = proj(wk, bk)
        v = proj(wv, bv)
        inv_freq = 1.0 / BASE ** (jnp.arange(0, HD, 2, dtype=jnp.float32) / HD)
        t = jnp.arange(s, dtype=jnp.float32)
        freqs = jnp.einsum('i,j->ij', t, inv_freq)
        emb = jnp.concatenate((freqs, freqs), axis=-1)
        cos = jnp.cos(emb)[None, None]
        sin = jnp.sin(emb)[None, None]
        q = q * cos + rotate_half(q) * sin
        k = k * cos + rotate_half(k) * sin
        scores = jnp.einsum('bhqd,bhkd->bhqk', q, k) / np.sqrt(HD).astype(np.float32)
        attn = jax.nn.softmax(scores, axis=-1)
        out = jnp.einsum('bhqk,bhkd->bhqd', attn, v)
        out = out.transpose(0, 2, 1, 3).reshape(b, s, HID)
        return out @ wo.T + bo

    def _L0_ffn_ref(x, q_w, k_w, v_w, o_w, sel_v_w, sel_o_w, route_scale):
        import jax, jax.numpy as jnp
        import numpy as np
        B, S, D = (2, 256, 128)
        H, E, P, K = (8, 8, 128, 2)
        SCALE = 1.0 / np.sqrt(P)

        def _get_sel_gate(x, w, route_scale):
            logits = jnp.einsum('bsd,ed->bse', x, w).astype(jnp.float32)
            raw = logits.reshape(x.shape[0], x.shape[1], H, E)
            probs = jax.nn.sigmoid(raw)
            vals, idx = jax.lax.top_k(probs, K)
            vals = vals / jnp.clip(vals.sum(-1, keepdims=True), 1e-09)
            vals = vals * route_scale
            gate = (jax.nn.one_hot(idx, E, dtype=vals.dtype) * vals[..., None]).sum(-2)
            return gate
        rs = route_scale[0]
        gate_v = _get_sel_gate(x, sel_v_w, rs)
        gate_o = _get_sel_gate(x, sel_o_w, rs)
        q = jnp.einsum('bsd,hpd->bhsp', x, q_w.reshape(H, P, D))
        k = jnp.einsum('bsd,hpd->bhsp', x, k_w.reshape(H, P, D))
        xv = jnp.einsum('bsd,hedp->bshep', x, v_w.reshape(H, E, D, P))
        v = jnp.einsum('bshep,bshe->bhsp', xv, gate_v)
        att = jax.nn.softmax(jnp.einsum('bhqp,bhkp->bhqk', q, k) * SCALE, axis=-1)
        ctx = jnp.einsum('bhqk,bhkp->bqhp', att, v)
        weighted = ctx[:, :, :, None, :] * gate_o[..., None]
        out = jnp.einsum('bshep,hepd->bsd', weighted, o_w.reshape(H, E, P, D))
        return out
    x = L0_attn_x
    xn = _layernorm(x, axis=-1)
    x = x + _L0_attn_ref(xn, L0_attn_wq, L0_attn_bq, L0_attn_wk, L0_attn_bk, L0_attn_wv, L0_attn_bv, L0_attn_wo, L0_attn_bo) + _L0_ffn_ref(xn, L0_ffn_q_w, L0_ffn_k_w, L0_ffn_v_w, L0_ffn_o_w, L0_ffn_sel_v_w, L0_ffn_sel_o_w, L0_ffn_route_scale)
    return x

_drawn_inputs = setup_inputs


def setup_inputs(seed=0):
    import zlib

    import numpy as np

    out = dict(_drawn_inputs(seed))
    spreads = {'L0_attn_bq': (0.0, 0.8),
     'L0_attn_bk': (0.0, 0.8),
     'L0_attn_bv': (0.0, 0.1),
     'L0_attn_bo': (0.0, 0.1)}
    factors = {}
    for name, (base, spread) in spreads.items():
        noise = np.random.default_rng([zlib.crc32(name.encode()), seed]).standard_normal(out[name].shape)
        drawn = base * np.exp(spread * noise) if base else spread * noise
        out[name] = jnp.asarray(drawn.astype(out[name].dtype))
    for name, factor in factors.items():
        out[name] = (out[name] * factor).astype(out[name].dtype)
    return out
```

```python
from contextlib import ExitStack

import concourse.bass as bass
from concourse import mybir

F32 = mybir.dt.float32
F32R = mybir.dt.float32r
ALU = mybir.AluOpType
ACT = mybir.ActivationFunctionType
AX_X = mybir.AxisListType.X

P = 128
B, S, D = 2, 1024, 128
NT = S // P
TT = B * NT
NH1, HD1 = 16, 8
SLOT = 32
GROUP = P // SLOT
NG = NH1 // GROUP
ROWS = 3 * HD1
H2, E2 = 8, 8
HALF = 512
TPH = HALF // P
EPS = 1e-5
SCALE1 = 1.0 / float(HD1) ** 0.5
SCALE2 = 1.0 / float(P) ** 0.5
NP = 4
RING = 3
PADS = 8
WA, WB = 2 * P + E2 * D, E2 * D

RING_INIT = B * 2 + TT
ST_A, ST_A_LAST = 3, 33
RING_A = RING_INIT + 4 * NT * 2 - 1
PER_ST_A, PER_RING_A = 36, 66
A_STEPS, F_STEPS = NG * B, H2 * B
ST_F = ST_A + PER_ST_A * (A_STEPS - 1) + ST_A_LAST + 2 - 1
RING_AO = RING_A + PER_RING_A * (A_STEPS - 1) + 3
RING_1 = RING_AO + 2 * TT // TPH
RING_F = RING_1 + 32 - 16
PER_ST_F, PER_RING_F = 12, 48
USED_F = A_STEPS * 16


def wait(eng, sem, value):
    if not isinstance(value, int) or value > 0:
        eng.wait_ge(sem, value)


def first(s):
    return isinstance(s, int) and s == 0


def ended(s):
    return isinstance(s, int) and s == F_STEPS - 1


def exp_fill(s, beat):
    prep = 0 if ended(s) else 2
    late = int(first(s)) if beat == 0 else 1
    return ST_F + PER_ST_F * s + prep + late + beat + int(beat > 4)


def den_fill(s, half):
    if half == 0:
        return exp_fill(s, 5) - 1
    return exp_fill(s, 7) + 1 if ended(s) else exp_fill(s + 1, 1) - 1


def moved_fill(s, k):
    return ST_F - 1 + k if first(s) else ST_F + PER_ST_F * (s - 1) + k + (1 if isinstance(s, int) and s == 1 else 0)


def queries_fill(t, half):
    if half:
        return ST_A + PER_ST_A * t + (2 if isinstance(t, int) and t == A_STEPS - 1 else 4)
    return 2 if first(t) else ST_A + PER_ST_A * (t - 1) + 21 + 2


def final(s):
    return isinstance(s, int) and s >= F_STEPS - B


def build(nc, x, w_in, wo_t, b_in, bo, rs, cos, sin, rank, wf, out):
    ctx = ExitStack()
    common, early, late = ExitStack(), ExitStack(), ExitStack()

    def sb(stack, name, shape, dt=F32):
        return stack.enter_context(nc.sbuf_tensor(name, shape, dt))

    def sem(name):
        return ctx.enter_context(nc.semaphore(name))

    acc = sb(common, "acc", [P, TT, D])
    x_hi = sb(common, "x_hi", [P, B * S], F32R)
    x_lo = sb(common, "x_lo", [P, B * S], F32R)
    gates = sb(common, "gates", [P, TT, 2 * H2 * E2])
    prob = sb(common, "prob", [P, NP, 2 * HALF])
    ident = sb(common, "ident", [P, P])
    neg_ident = sb(common, "neg_ident", [P, P])
    ones = sb(common, "ones", [P, P])
    ones_r = sb(common, "ones_r", [P, P], F32R)
    pad = sb(common, "pad", [P, PADS])
    rs_b = sb(common, "rs_b", [P, 1])
    xn = sb(early, "xn", [P, TT, D])
    xt = sb(early, "xt", [P, B * S])
    w_in_s = sb(early, "w_in_s", [P, 4 * P])
    wo_s = sb(early, "wo_s", [P, P])
    b_in_s = sb(early, "b_in_s", [P, 3 * P])
    bo_s = sb(early, "bo_s", [P, P])
    cos_s = sb(early, "cos_s", [P, NT, HD1])
    sin_s = sb(early, "sin_s", [P, NT, HD1])
    rank_s = sb(early, "rank_s", [P, E2])
    stats = sb(early, "stats", [P, TT, 6])
    mv = sb(early, "mv", [P, TT, 2])
    rstd = sb(early, "rstd", [P, TT])
    newton = sb(early, "newton", [P, TT])
    qk_tok = sb(early, "qk_tok", [P, TT, 2 * P])
    v_tok = sb(early, "v_tok", [P, TT, P])
    t_a = sb(early, "t_a", [P, TT * D])
    t_b = sb(early, "t_b", [P, TT * D])
    small = sb(early, "small", [P, 6, TT * 2 * H2])
    qs = [sb(early, f"qs{i}", [P, NT, P]) for i in range(2)]
    ks = [sb(early, f"ks{i}", [P, NT, P]) for i in range(2)]
    q_t = [sb(early, f"q_t{i}", [P, GROUP, S], F32R) for i in range(2)]
    k_t = [sb(early, f"k_t{i}", [P, S], F32R) for i in range(2)]
    v_st = [sb(early, f"v_st{i}", [P, NT, GROUP, SLOT]) for i in range(2)]
    mx1 = [sb(early, f"mx1{i}", [P, NT, GROUP, 2]) for i in range(2)]
    o_t = sb(early, "o_t", [P, 2, HALF])
    rden1 = sb(early, "rden1", [P, 2, TPH, GROUP])
    early.close()
    raw_a = sb(late, "raw_a", [P, WA])
    raw_b = sb(late, "raw_b", [P, WB])
    a_hi = [sb(late, f"a_hi{i}", [P, WA], F32R) for i in range(2)]
    a_lo = [sb(late, f"a_lo{i}", [P, WA], F32R) for i in range(2)]
    b_hi = [sb(late, f"b_hi{i}", [P, WB], F32R) for i in range(2)]
    b_lo = [sb(late, f"b_lo{i}", [P, WB], F32R) for i in range(2)]
    qk_f = sb(late, "qk_f", [P, 2, S])
    qk_hi = [sb(late, f"qk_hi{i}", [P, 2, S], F32R) for i in range(2)]
    qk_lo = [sb(late, f"qk_lo{i}", [P, 2, S], F32R) for i in range(2)]
    v_acc = [sb(late, f"v_acc{i}", [P, NT, P]) for i in range(2)]
    diag = [sb(late, f"diag{i}", [P, NT, P], F32R) for i in range(2)]
    mx2 = sb(late, "mx2", [P, NT, 2])
    m2 = sb(late, "m2", [P, NT])
    p_sum = sb(late, "p_sum", [P, 2, 2 * HALF])
    ctx_f = sb(late, "ctx_f", [P, HALF])
    ctx_hi = sb(late, "ctx_hi", [P, S], F32R)
    ctx_lo = sb(late, "ctx_lo", [P, S], F32R)
    den = sb(late, "den", [P, NT])
    rden = sb(late, "rden", [P, NT])
    gv = sb(late, "gv", [P, NT, E2])
    go = sb(late, "go", [P, NT, E2])
    late.close()
    common.close()

    st = [ctx.enter_context(nc.psum_tensor(f"st{i}", [P, 2 * HALF], F32)) for i in range(2)]
    ring = [ctx.enter_context(nc.psum_tensor(f"ring{i}", [P, HALF], F32)) for i in range(RING)]
    pv = ctx.enter_context(nc.psum_tensor("pv", [P, HALF], F32))

    x_loaded, w_loaded = [sem(f"x_loaded{b}") for b in range(B)], sem("w_loaded")
    raw_a_loaded, raw_b_loaded, stored = sem("raw_a_loaded"), sem("raw_b_loaded"), sem("stored")
    consts_made, memset_done = sem("consts_made"), sem("memset_done")
    st_filled, st_freed = sem("st_filled"), sem("st_freed")
    ring_filled, ring_freed = sem("ring_filled"), sem("ring_freed")
    prob_used, prob_summed = sem("prob_used"), sem("prob_summed")
    var_made, sqrt_made = sem("var_made"), sem("sqrt_made")
    xn_made, x_hi_made, x_lo_made = sem("xn_made"), sem("x_hi_made"), sem("x_lo_made")
    tok_made, ex_made = sem("tok_made"), sem("ex_made")
    stack_made, v_stack_made = sem("stack_made"), sem("v_stack_made")
    max_made, o_t_made = sem("max_made"), sem("o_t_made")
    wa_hi_made, wa_split, wb_hi_made, wb_split = sem("wa_hi_made"), sem("wa_split"), sem("wb_hi_made"), sem("wb_split")
    qk_split, diag_made = sem("qk_split"), sem("diag_made")
    ctx_hi_made, ctx_split = sem("ctx_hi_made"), sem("ctx_split")
    prob_total, den_used = sem("prob_total"), sem("den_used")
    pool_step, stack_step, dve_step = sem("pool_step"), sem("stack_step"), sem("dve_step")

    block = ctx.enter_context(nc.Block())

    def tiles(b, half=0):
        t = b * NT + half * TPH
        return slice(t, t + TPH)

    @block.sync
    def _(sp):
        for b in range(B):
            sp.dma_start(acc[:, b * NT:(b + 1) * NT, :], x[b].rearrange("(t p) d -> p t d", p=P)).then_inc(x_loaded[b], 16)
        sp.dma_start(w_in_s[:, :], w_in).then_inc(w_loaded, 16)
        sp.dma_start(b_in_s[:, :], b_in.rearrange("(a n) -> a n", a=1).broadcast_to([P, 3 * P])).then_inc(w_loaded, 16)
        sp.dma_start(cos_s[:, :, :], cos.rearrange("(t p) e -> p t e", p=P)).then_inc(w_loaded, 16)
        sp.dma_start(sin_s[:, :, :], sin.rearrange("(t p) e -> p t e", p=P)).then_inc(w_loaded, 16)
        sp.dma_start(rank_s[:, :], rank.rearrange("(a n) -> a n", a=1).broadcast_to([P, E2])).then_inc(w_loaded, 16)
        sp.dma_start(bo_s[:, :], bo.rearrange("(a n) -> a n", a=1).broadcast_to([P, P])).then_inc(w_loaded, 16)
        sp.dma_start(rs_b[:, :], rs.rearrange("(a n) -> a n", a=1).broadcast_to([P, 1])).then_inc(w_loaded, 16)
        sp.dma_start(wo_s[:, :], wo_t).then_inc(w_loaded, 16)
        sp.wait_ge(ring_freed, RING_1)
        sp.dma_start(raw_a[:, :], wf[0, :, 0:WA]).then_inc(raw_a_loaded, 16)
        sp.dma_start(raw_b[:, :], wf[0, :, WA:WA + WB]).then_inc(raw_b_loaded, 16)
        with sp.Fori(1, H2) as h:
            sp.wait_ge(wa_split, h)
            sp.dma_start(raw_a[:, :], wf[bass.ds(h, 1), :, 0:WA].rearrange("a p n -> p (a n)")).then_inc(raw_a_loaded, 16)
            sp.wait_ge(wb_split, h)
            sp.dma_start(raw_b[:, :], wf[bass.ds(h, 1), :, WA:WA + WB].rearrange("a p n -> p (a n)")).then_inc(raw_b_loaded, 16)
        for b in range(B):
            sp.wait_ge(ring_freed, RING_F + PER_RING_F * (F_STEPS - 1) + 16 * (b + 1))
            sp.dma_start(out[b].rearrange("(t p) d -> p t d", p=P), acc[:, b * NT:(b + 1) * NT, :]).then_inc(stored, 16)
        sp.wait_ge(stored, 16 * B)


    @block.gpsimd
    def _(pool):
        links = [0]

        def link(ins):
            links[0] += 1
            ins.then_inc(pool_step, 1)
            pool.wait_ge(pool_step, links[0])

        pads = [0]

        def stand_alone():
            pads[0] = (pads[0] + 1) % PADS
            pool.tensor_tensor(pad[:, pads[0]:pads[0] + 1], ones[:, 0:1], ones[:, 0:1], ALU.mult)

        pool.memset(ones[:, :], 1.0)
        for i in range(2):
            pool.memset(qs[i][:, :, :], 0.0)
            pool.memset(ks[i][:, :, :], 0.0)
            pool.memset(v_st[i][:, :, :, :], 0.0)
            pool.memset(q_t[i][:, :, :].bitcast(F32), 0.0)
        link(pool.memset(ident[:, :], 0.0))
        for i in range(2):
            for j in range(GROUP):
                pool.memset(ks[i][:, :, j * SLOT + ROWS:j * SLOT + ROWS + 1], -1.0)
                pool.memset(v_st[i][:, :, j, HD1:HD1 + 1], 1.0)
        link(pool.affine_select(out=ident[:, :], in_=ident[:, :], compare_op=ALU.not_equal, fill=1.0, base=0,
                                pattern=[[-1, P]], channel_multiplier=1))
        pool.tensor_copy(ones_r[:, :], ones[:, :])
        pool.tensor_scalar(neg_ident[:, :], ident[:, :], -1.0, None, ALU.mult).then_inc(consts_made, 1)

        for n in range(B * 2):
            cols = slice(n * HALF, (n + 1) * HALF)
            pool.wait_ge(x_hi_made, n + 1)
            pool.tensor_tensor(x_lo[:, cols], xt[:, cols], x_hi[:, cols], ALU.subtract).then_inc(x_lo_made, 1)

        def heads(src, b, g, off):
            a = src[:, b * NT:(b + 1) * NT, bass.ds(g * (GROUP * HD1) + off, GROUP * HD1)]
            return a.rearrange("p t (j e) -> p t j e", e=HD1)

        def make_stack(u, g, i):
            if isinstance(u, int) and u < 2:
                pool.wait_ge(tok_made, i + 1)
            else:
                pool.wait_ge(st_freed, ST_A + PER_ST_A * (u - 2) + 5)
                stand_alone()

            def part(buf, k):
                a = buf[:, :, :].rearrange("p t (j r) -> p t j r", r=SLOT)
                return a[:, :, :, k * HD1:(k + 1) * HD1]

            q, k = heads(qk_tok, i, g, 0), heads(qk_tok, i, g, P)
            pool.memset(qs[i][:, :, :].rearrange("p t (j r) -> p t j r", r=SLOT)[:, :, :, ROWS:ROWS + 1], 0.0)
            pool.tensor_copy(part(qs[i], 0).bitcast(F32R), q)
            pool.tensor_copy(part(ks[i], 0).bitcast(F32R), k)
            pool.tensor_copy(part(qs[i], 2).bitcast(F32R), q)
            ins = pool.tensor_copy(part(ks[i], 1).bitcast(F32R), k)
            ins.then_inc(stack_step, 1)
            pool.wait_ge(stack_step, u + 1)
            stand_alone()
            pool.tensor_tensor(part(qs[i], 1).bitcast(F32R), q, part(qs[i], 0), ALU.subtract)
            pool.tensor_tensor(part(ks[i], 2).bitcast(F32R), k, part(ks[i], 0), ALU.subtract).then_inc(stack_made, 1)

        def make_values(u, g, i):
            wait(pool, prob_used, 16 * (u - 1))
            stand_alone()
            pool.tensor_copy(v_st[i][:, :, :, 0:HD1], heads(v_tok, i, g, 0)).then_inc(v_stack_made, 1)

        make_stack(0, 0, 0)
        make_values(0, 0, 0)
        make_stack(1, 0, 1)
        pool.tensor_copy(v_st[1][:, :, :, 0:HD1], heads(v_tok, 1, 0, 0)).then_inc(v_stack_made, 1)
        make_stack(2, 1, 0)
        with pool.Fori(0, 2) as it:
            make_values(2 * it + 2, it + 1, 0)
            make_stack(2 * it + 3, it + 1, 1)
            make_values(2 * it + 3, it + 1, 1)
            make_stack(2 * it + 4, it + 2, 0)
        make_values(6, 3, 0)
        make_stack(7, 3, 1)
        make_values(7, 3, 1)

        pool.wait_ge(ring_freed, RING_1)

        def split_a(h, i):
            pool.wait_ge(wa_hi_made, h + 1)
            pool.tensor_tensor(a_lo[i][:, :], raw_a[:, :], a_hi[i][:, :], ALU.subtract).then_inc(wa_split, 1)

        def split_b(h, i):
            pool.wait_ge(wb_hi_made, h + 1)
            pool.tensor_tensor(b_lo[i][:, :], raw_b[:, :], b_hi[i][:, :], ALU.subtract).then_inc(wb_split, 1)

        def split_qk(s, i):
            for k in range(2):
                pool.wait_ge(st_freed, moved_fill(s, k) + 1)
                pool.tensor_tensor(qk_lo[i][:, k, :], qk_f[:, k, :], qk_hi[i][:, k, :], ALU.subtract).then_inc(qk_split, 1)

        def step(s, r, h, last=False):
            if not last:
                split_qk(s + 1, (r + 1) % 2)
            for beat in range(8):
                half, n = beat // 4, beat % 4
                pool.wait_ge(st_freed, exp_fill(s, beat) + 1)
                if n == 0:
                    if not first(s):
                        pool.wait_ge(st_freed, den_fill(s - 1, half) + 1)
                    stand_alone()
                    ins = pool.tensor_copy(p_sum[:, half, :], prob[:, beat % NP, :])
                else:
                    pool.wait_ge(prob_summed, 8 * s + beat)
                    ins = pool.tensor_tensor(p_sum[:, half, :], p_sum[:, half, :], prob[:, beat % NP, :], ALU.add)
                ins.then_inc(prob_summed, 1)
                if n == 3:
                    pool.wait_ge(prob_summed, 8 * s + beat + 1)
                    pool.tensor_tensor(p_sum[:, half, 0:HALF], p_sum[:, half, 0:HALF], p_sum[:, half, HALF:],
                                       ALU.add).then_inc(prob_total, 1)
                    cols = slice(half * HALF, (half + 1) * HALF)
                    pool.wait_ge(ctx_hi_made, 2 * s + half + 1)
                    pool.tensor_tensor(ctx_lo[:, cols], ctx_f[:, :], ctx_hi[:, cols], ALU.subtract).then_inc(ctx_split, 1)
                if beat == 1 and not final(s):
                    (split_b if r % 2 else split_a)(h + 1, (r // 2 + 1) % 2)

        split_a(0, 0)
        split_b(0, 0)
        split_qk(0, 0)
        step(0, 0, 0)
        step(1, 1, 0)
        with pool.Fori(0, 3) as it:
            for r in range(2, 6):
                step(4 * it + r, r, 2 * it + r // 2)
        for s in range(14, F_STEPS):
            step(s, s % 4, s // 2, last=s == F_STEPS - 1)

    @block.scalar
    def _(act):
        for b in range(B):
            act.wait_ge(var_made, b + 1)
            ts = slice(b * NT, (b + 1) * NT)
            act.activation(rstd[:, ts], mv[:, ts, 1:2].rearrange("p t a -> p (t a)"), ACT.Sqrt).then_inc(sqrt_made, 1)
        for n in range(B * 2):
            cols = slice(n * HALF, (n + 1) * HALF)
            act.wait_ge(ring_freed, n // 2 * (2 + NT) + n % 2 + 1)
            act.activation(x_hi[:, cols], xt[:, cols], ACT.Copy).then_inc(x_hi_made, 1)
        act.wait_ge(tok_made, B)
        act.activation(gates[:, :, :], gates[:, :, :], ACT.Exp, scale=-1.0).then_inc(ex_made, 1)

        def move_heads(bank, i, cols):
            for j in range(GROUP):
                rows = slice(j * SLOT, (j + 1) * SLOT)
                ins = act.activation(q_t[i][rows, j, cols], bank[rows, 0:cols.stop - cols.start], ACT.Copy)
            ins.then_inc(st_freed, 1)

        def move_stacks(base, odd, n, i):
            act.wait_ge(st_filled, base + n + 1)
            act.activation(k_t[i][:, :], st[(odd + n) % 2][:, :], ACT.Copy).then_inc(st_freed, 1)
            act.wait_ge(st_filled, base + n + 2)
            move_heads(st[(odd + n + 1) % 2], i, slice(0, S))

        def move_queries(base, odd, n, i, half):
            act.wait_ge(st_filled, base + n + 1)
            move_heads(st[(odd + n) % 2], i, slice(half * HALF, (half + 1) * HALF))

        def att_step(t, i, prep=True):
            base, n = ST_A + PER_ST_A * t, 0
            if prep:
                move_stacks(base, ST_A, n, 1 - i)
                n += 2
            for beat in range(16):
                if beat == 1:
                    move_queries(base, ST_A, n, i, 1)
                    n += 1
                if beat == 9 and prep:
                    move_queries(base, ST_A, n, 1 - i, 0)
                    n += 1
                wait(act, prob_used, 16 * t + beat - 1)
                for pair in range(2):
                    act.wait_ge(st_filled, base + n + 1)
                    act.activation(prob[:, 2 * (beat % 2) + pair, :], st[(ST_A + n) % 2][:, :], ACT.Exp,
                                   scale=SCALE1).then_inc(st_freed, 1)
                    n += 1
                if beat % 8 == 7:
                    half = beat // 8
                    act.wait_ge(prob_used, 16 * t + 8 * half + 8)
                    act.activation(o_t[:, half, :], pv[:, :], ACT.Copy).then_inc(o_t_made, 1)

        move_stacks(0, 0, 0, 0)
        move_queries(0, 0, 2, 0, 0)
        att_step(0, 0)
        with act.Fori(0, 3) as it:
            att_step(2 * it + 1, 1)
            att_step(2 * it + 2, 0)
        att_step(A_STEPS - 1, 1, prep=False)

        act.wait_ge(ring_freed, RING_1)

        def head_a(h, i):
            act.wait_ge(raw_a_loaded, 16 * h + 16)
            act.activation(a_hi[i][:, :], raw_a[:, :], ACT.Copy).then_inc(wa_hi_made, 1)

        def head_b(h, i):
            act.wait_ge(raw_b_loaded, 16 * h + 16)
            act.activation(b_hi[i][:, :], raw_b[:, :], ACT.Copy).then_inc(wb_hi_made, 1)

        def move_qk(s, i, base, odd, n):
            for k in range(2):
                act.wait_ge(st_filled, base + n + k + 1)
                wait(act, qk_split, 2 * s + k - 1)
                act.activation(qk_f[:, k, :], st[(odd + n + k) % 2][:, :], ACT.Copy)
                act.activation(qk_hi[i][:, k, :], st[(odd + n + k) % 2][:, :],
                               ACT.Copy).then_inc(st_freed, 1)

        def move_den(s, half, base, n):
            act.wait_ge(st_filled, base + n + 1)
            wait(act, den_used, 2 * s - 1 + half)
            act.activation(den[:, half * TPH:(half + 1) * TPH], st[(ST_F + n) % 2][:, 0:TPH],
                           ACT.Copy).then_inc(st_freed, 1)

        def step(s, r, h, last=False):
            i = r % 2
            base, n = ST_F + PER_ST_F * s, int(first(s))
            if not last:
                move_qk(s + 1, 1 - i, base, ST_F, n)
                n += 2
            for beat in range(8):
                if beat == 1 and not first(s):
                    move_den(s - 1, 1, base, n)
                    n += 1
                if beat == 5:
                    move_den(s, 0, base, n)
                    n += 1
                act.wait_ge(prob_used, USED_F + (8 * s + beat - 3 if beat > 2 or not first(s) else 0))
                wait(act, prob_summed, 8 * s + beat - 3)
                act.wait_ge(st_filled, base + n + 1)
                act.activation(prob[:, beat % NP, :], st[(ST_F + n) % 2][:, :], ACT.Exp,
                               scale=SCALE2).then_inc(st_freed, 1)
                n += 1
                if beat % 4 == 3:
                    half = beat // 4
                    act.wait_ge(prob_used, USED_F + 8 * s + beat + 1)
                    wait(act, ctx_split, 2 * s + half)
                    act.activation(ctx_f[:, :], pv[:, :], ACT.Copy)
                    act.activation(ctx_hi[:, half * HALF:(half + 1) * HALF], pv[:, :], ACT.Copy).then_inc(ctx_hi_made, 1)
                if beat == 1 and not final(s):
                    (head_b if r % 2 else head_a)(h + 1, (r // 2 + 1) % 2)
            return n

        head_a(0, 0)
        head_b(0, 0)
        move_qk(0, 0, ST_F - 1, ST_F - 1, 0)
        step(0, 0, 0)
        step(1, 1, 0)
        with act.Fori(0, 3) as it:
            for r in range(2, 6):
                step(4 * it + r, r, 2 * it + r // 2)
        for s in range(14, F_STEPS):
            n = step(s, s % 4, s // 2, last=s == F_STEPS - 1)
        move_den(F_STEPS - 1, 1, ST_F + PER_ST_F * (F_STEPS - 1), n)

    @block.tensor
    def _(pe):
        pe.wait_ge(consts_made, 1)
        n = 0
        for b in range(B):
            for half in range(2):
                pe.wait_ge(xn_made, 2 * b + half + 1)
                wait(pe, ring_freed, n - 2)
                for c in range(TPH):
                    ins = pe.transpose(ring[n % RING][:, c * P:(c + 1) * P], xn[:, b * NT + half * TPH + c, :], ident[:, :])
                ins.then_inc(ring_filled, 1)
                n += 1
            if b == 0:
                pe.wait_ge(w_loaded, 16 * 8)
            for t in range(b * NT, (b + 1) * NT):
                pe.wait_ge(ring_freed, b * (2 + NT) + t % NT // TPH + 1)
                wait(pe, ring_freed, n - 2)
                pe.matmul(ring[n % RING][:, :], xt[:, t * P:(t + 1) * P], w_in_s[:, :],
                          start=True, stop=True).then_inc(ring_filled, 1)
                n += 1

        def turn_stacks(u, base, odd, n, i):
            pe.wait_ge(stack_made, u + 1)
            for k, buf in enumerate((ks[i], qs[i])):
                wait(pe, st_freed, base + n + k - 1)
                for c in range(NT):
                    ins = pe.transpose(st[(odd + n + k) % 2][:, c * P:(c + 1) * P], buf[:, c, :], ident[:, :])
                ins.then_inc(st_filled, 1)

        def turn_queries(u, base, odd, n, i, half):
            pe.wait_ge(max_made, 2 * u + half + 1)
            pe.wait_ge(st_freed, base + n - 1)
            for c in range(TPH):
                ins = pe.transpose(st[(odd + n) % 2][:, c * P:(c + 1) * P], qs[i][:, half * TPH + c, :], ident[:, :])
            ins.then_inc(st_filled, 1)

        def query_scores(base, odd, n, i, part, q):
            tile, k, j = part // 2, q // 2, 2 * (part % 2) + q % 2
            wait(pe, ring_freed, base + n - 2)
            pe.matmul(ring[(odd + n) % RING][:, :], q_t[i][:, j, tile * P:(tile + 1) * P],
                      k_t[i][:, k * HALF:(k + 1) * HALF], start=True, stop=True).then_inc(ring_filled, 1)
            return n + 1

        def turn_output(t, base, odd, n, half):
            pe.wait_ge(o_t_made, 2 * t + half + 1)
            pe.wait_ge(ring_freed, base + n - 2)
            for c in range(TPH):
                ins = pe.transpose(ring[(odd + n) % RING][:, c * P:(c + 1) * P], o_t[:, half, c * P:(c + 1) * P], ident[:, :])
            ins.then_inc(ring_filled, 1)
            return n + 1

        def att_values(t, i, beat, made):
            half, kt = beat // 8, beat % 8
            if kt == 0:
                wait(pe, o_t_made, 2 * t + half)
                pe.wait_ge(v_stack_made, t + 1)
            pe.wait_ge(st_freed, made)
            for j in range(GROUP):
                ins = pe.matmul(pv[j * SLOT:(j + 1) * SLOT, :], v_st[i][:, kt, j, :],
                                prob[:, 2 * (beat % 2) + j // 2, (j % 2) * HALF:(j % 2 + 1) * HALF],
                                start=kt == 0, stop=kt == NT - 1)
            ins.then_inc(prob_used, 1)

        def att_step(t, i, prep=True):
            sb_, s_n = ST_A + PER_ST_A * t, 0
            rb, r_n = RING_A + PER_RING_A * t, int(first(t))
            if prep:
                turn_stacks(t + 1, sb_, ST_A, s_n, 1 - i)
                s_n += 2
            for beat in range(16):
                half, kt = beat // 8, beat % 8
                if beat == 1:
                    turn_queries(t, sb_, ST_A, s_n, i, 1)
                    s_n += 1
                    if not first(t):
                        r_n = turn_output(t - 1, rb, RING_A, r_n, 1)
                if beat == 9:
                    if prep:
                        turn_queries(t + 1, sb_, ST_A, s_n, 1 - i, 0)
                        s_n += 1
                    r_n = turn_output(t, rb, RING_A, r_n, 0)
                if kt == 0:
                    pe.wait_ge(st_freed, queries_fill(t, half) + 1)
                if prep and beat == 0:
                    pe.wait_ge(st_freed, sb_ + 2)
                for j in range(GROUP):
                    if j % 2 == 0:
                        pe.wait_ge(st_freed, sb_ + s_n - 1)
                    ins = pe.matmul(st[(ST_A + s_n) % 2][:, (j % 2) * HALF:(j % 2 + 1) * HALF],
                                    k_t[i][:, kt * P:(kt + 1) * P], q_t[i][:, j, half * HALF:(half + 1) * HALF],
                                    start=True, stop=True)
                    if j % 2:
                        ins.then_inc(st_filled, 1)
                        s_n += 1
                    if prep and j:
                        r_n = query_scores(rb, RING_A, r_n, 1 - i, beat, j - 1)
                if beat:
                    att_values(t, i, beat - 1, made)
                if prep:
                    r_n = query_scores(rb, RING_A, r_n, 1 - i, beat, 3)
                made = sb_ + s_n
            att_values(t, i, 15, made)
            return rb, r_n

        turn_stacks(0, 0, 0, 0, 0)
        pe.wait_ge(st_freed, 2)
        n = 0
        for part in range(16):
            for q in range(4):
                n = query_scores(RING_INIT, RING_INIT, n, 0, part, q)
            if part == 7:
                turn_queries(0, 0, 0, 2, 0, 0)
        att_step(0, 0)
        with pe.Fori(0, 3) as it:
            att_step(2 * it + 1, 1)
            att_step(2 * it + 2, 0)
        rb, n = att_step(A_STEPS - 1, 1, prep=False)
        n = rb + turn_output(A_STEPS - 1, rb, rb, n, 1)

        for q in range(TT // TPH):
            if q == 0:
                pe.wait_ge(ring_freed, RING_AO)
            pe.wait_ge(ring_freed, n - 2)
            for c in range(TPH):
                ins = pe.transpose(ring[n % RING][:, c * P:(c + 1) * P], xn[:, q * TPH + c, :], ident[:, :])
            ins.then_inc(ring_filled, 1)
            n += 1
        for q in range(TT // TPH):
            pe.wait_ge(ring_freed, RING_AO + q + 1)
            pe.wait_ge(ring_freed, n - 2)
            for c in range(TPH):
                t = q * TPH + c
                ins = pe.matmul(ring[n % RING][:, c * P:(c + 1) * P], xt[:, t * P:(t + 1) * P], wo_s[:, :],
                                start=True, stop=True)
            ins.then_inc(ring_filled, 1)
            n += 1
        assert n == RING_1

        def product(out, l_hi, l_lo, r_hi, r_lo, more=False):
            pe.matmul(out, l_hi, r_hi, start=True, stop=False)
            pe.matmul(out, l_lo, r_hi, start=False, stop=False)
            return pe.matmul(out, l_hi, r_lo, start=False, stop=not more)

        def project(s, i, hp, base, odd, n):
            for k in range(2):
                pe.wait_ge(st_freed, base + n + k - 1)
                w = slice((1 - k) * P, (2 - k) * P)
                for half in range(2):
                    cols = slice(i * S + half * HALF, i * S + (half + 1) * HALF)
                    ins = product(st[(odd + n + k) % 2][:, half * HALF:(half + 1) * HALF], a_hi[hp][:, w], a_lo[hp][:, w],
                                  x_hi[:, cols], x_lo[:, cols])
                ins.then_inc(st_filled, 1)

        def experts(base, odd, n, l_hi, l_lo, tile, r_hi, r_lo, half):
            rows = slice(tile * P, (tile + 1) * P)
            pe.wait_ge(ring_freed, base + n - 2)
            product(ring[(odd + n) % RING][:, :], l_hi[:, rows], l_lo[:, rows], r_hi[:, half], r_lo[:, half]).then_inc(ring_filled, 1)
            return n + 1

        def values(base, odd, n, i, hp, beat, e):
            half = slice(2 * P + e * HALF, 2 * P + (e + 1) * HALF)
            return experts(base, odd, n, x_hi, x_lo, i * NT + beat, a_hi[hp], a_lo[hp], half)

        def outputs(base, odd, n, hp, beat, e):
            return experts(base, odd, n, ctx_hi, ctx_lo, beat, b_hi[hp], b_lo[hp], slice(e * HALF, (e + 1) * HALF))

        def maxima(base, odd, n, i, tile, k):
            pe.wait_ge(ring_freed, base + n - 2)
            pe.matmul(ring[(odd + n) % RING][:, :], qk_hi[i][:, 1, tile * P:(tile + 1) * P],
                      qk_hi[i][:, 0, k * HALF:(k + 1) * HALF], start=True, stop=True).then_inc(ring_filled, 1)
            return n + 1

        def denominators(s, half, base, odd, n):
            pe.wait_ge(prob_total, 2 * s + half + 1)
            pe.wait_ge(st_freed, base + n - 1)
            for c in range(TPH):
                ins = pe.matmul(st[(odd + n) % 2][:, c:c + 1], p_sum[:, half, c * P:(c + 1) * P], ones[:, 0:1],
                                start=True, stop=True)
            ins.then_inc(st_filled, 1)
            return n + 1

        def step(s, r, h, prep=True):
            i, post = r % 2, not first(s)
            nh, ph = (r + 1) // 2 % 2, (r - 1) // 2 % 2
            sb_, s_n = ST_F + PER_ST_F * s, int(first(s))
            rb, r_n = RING_F + PER_RING_F * s, 16 * int(first(s))
            if prep:
                if i:
                    pe.wait_ge(wa_split, h + 2)
                project(s + 1, 1 - i, nh, sb_, ST_F, s_n)
                s_n += 2
            for beat in range(8):
                half, n = beat // 4, beat % 4
                if beat == 1 and post:
                    s_n = denominators(s - 1, 1, sb_, ST_F, s_n)
                if beat == 5:
                    s_n = denominators(s, 0, sb_, ST_F, s_n)
                if post and n == 0:
                    if i == 1 and half == 0:
                        pe.wait_ge(wb_split, h + 1)
                    pe.wait_ge(ctx_split, 2 * s - 1 + half)
                if prep:
                    r_n = values(rb, RING_F, r_n, 1 - i, nh, beat, 0)
                if post:
                    r_n = outputs(rb, RING_F, r_n, ph, beat, 0)
                if prep:
                    r_n = values(rb, RING_F, r_n, 1 - i, nh, beat, 1)
                if n == 0:
                    pe.wait_ge(diag_made, 2 * s + half + 1)
                pe.wait_ge(st_freed, sb_ + s_n - 1)
                cols = slice(half * HALF, (half + 1) * HALF)
                for k in range(2):
                    rows = slice((2 * n + k) * P, (2 * n + k + 1) * P)
                    out = st[(ST_F + s_n) % 2][:, k * HALF:(k + 1) * HALF]
                    product(out, qk_hi[i][:, 0, rows], qk_lo[i][:, 0, rows], qk_hi[i][:, 1, cols], qk_lo[i][:, 1, cols], more=True)
                    ins = pe.matmul(out, ones_r[:, :], diag[i][:, half * TPH:(half + 1) * TPH, :], start=False, stop=True)
                ins.then_inc(st_filled, 1)
                s_n += 1
                if post:
                    r_n = outputs(rb, RING_F, r_n, ph, beat, 1)
                if prep:
                    if beat == 0:
                        pe.wait_ge(qk_split, 2 * s + 4)
                    r_n = maxima(rb, RING_F, r_n, 1 - i, beat, 0)
                if n == 0:
                    if first(s) and half == 0:
                        pe.wait_ge(o_t_made, 2 * A_STEPS)
                    else:
                        pe.wait_ge(ctx_hi_made, 2 * s + half)
                    pe.wait_ge(ring_freed, rb + 16 * int(first(s)))
                pe.wait_ge(st_freed, sb_ + s_n)
                for k in range(2):
                    ins = pe.matmul(pv[:, :], v_acc[i][:, 2 * n + k, :], prob[:, beat % NP, k * HALF:(k + 1) * HALF],
                                    start=n == 0 and k == 0, stop=n == 3 and k == 1)
                ins.then_inc(prob_used, 1)
                if prep:
                    r_n = maxima(rb, RING_F, r_n, 1 - i, beat, 1)
            return sb_, s_n, rb, r_n

        pe.wait_ge(wa_split, 1)
        project(0, 0, 0, ST_F - 1, ST_F - 1, 0)
        pe.wait_ge(qk_split, 2)
        n = 0
        for beat in range(8):
            for e in range(2):
                n = values(RING_1, RING_1, n, 0, 0, beat, e)
            for k in range(2):
                n = maxima(RING_1, RING_1, n, 0, beat, k)
        step(0, 0, 0)
        step(1, 1, 0)
        with pe.Fori(0, 3) as it:
            for r in range(2, 6):
                step(4 * it + r, r, 2 * it + r // 2)
        for s in range(14, F_STEPS):
            sb_, s_n, rb, r_n = step(s, s % 4, s // 2, prep=s < F_STEPS - 1)
        denominators(F_STEPS - 1, 1, sb_, ST_F, s_n)
        for beat in range(8):
            if beat % 4 == 0:
                pe.wait_ge(ctx_split, 2 * (F_STEPS - 1) + beat // 4 + 1)
            for e in range(2):
                r_n = outputs(rb, RING_F, r_n, (H2 - 1) % 2, beat, e)

    @block.vector
    def _(dve):
        chain = [0, 0]

        def mark(ins):
            chain[1] += 1
            return ins.then_inc(dve_step, 1)

        def settle(but=0):
            dve.wait_ge(dve_step, chain[0] + chain[1] - but)

        def then(ins):
            mark(ins)
            settle()

        n = 0
        for b in range(B):
            dve.wait_ge(x_loaded[b], 16)
            ts = slice(b * NT, (b + 1) * NT)
            for t in range(b * NT, (b + 1) * NT):
                ins = dve.bn_stats(stats[:, t, :], acc[:, t, :])
            mark(ins)
            settle()
            for t in range(b * NT, (b + 1) * NT):
                ins = dve.bn_aggr(mv[:, t, :], stats[:, t, :])
            mark(ins)
            settle()
            var = mv[:, ts, 1:2].rearrange("p t a -> p (t a)")
            dve.tensor_scalar(var, var, EPS, None, ALU.add).then_inc(var_made, 1)
            dve.wait_ge(sqrt_made, b + 1)
            r, z = rstd[:, ts], newton[:, ts]
            then(dve.reciprocal(r, r))
            then(dve.tensor_tensor(z, r, r, ALU.mult))
            then(dve.tensor_tensor(z, z, var, ALU.mult))
            then(dve.tensor_scalar(z, z, -0.5, 1.5, ALU.mult, ALU.add))
            then(dve.tensor_tensor(r, r, z, ALU.mult))
            for t in range(b * NT, (b + 1) * NT):
                ins = dve.tensor_scalar(xn[:, t, :], acc[:, t, :], mv[:, t, 0:1], rstd[:, t:t + 1], ALU.subtract, ALU.mult)
                if t % TPH == TPH - 1:
                    ins.then_inc(xn_made, 1)
            for half in range(2):
                dve.wait_ge(ring_filled, n + 1)
                cols = slice(b * S + half * HALF, b * S + (half + 1) * HALF)
                dve.tensor_copy(xt[:, cols], ring[n % RING][:, :]).then_inc(ring_freed, 1)
                n += 1
            if b == 0:
                dve.wait_ge(w_loaded, 16 * 8)
            for t in range(b * NT, (b + 1) * NT):
                dve.wait_ge(ring_filled, n + 1)
                bank = ring[n % RING]
                dve.tensor_tensor(qk_tok[:, t, :], bank[:, 0:2 * P], b_in_s[:, 0:2 * P], ALU.add)
                dve.tensor_tensor(v_tok[:, t, :], bank[:, 2 * P:3 * P], b_in_s[:, 2 * P:3 * P], ALU.add)
                dve.tensor_copy(gates[:, t, :], bank[:, 3 * P:4 * P]).then_inc(ring_freed, 1)
                n += 1
            dve.wait_ge(ring_freed, n)
            for k in range(2):
                v = qk_tok[:, ts, k * P:(k + 1) * P].rearrange("p t (h e) -> p t h e", e=HD1)
                a = t_a[:, k * S:(k + 1) * S].rearrange("p (t h e) -> p t h e", h=NH1, e=HD1)
                c = t_b[:, k * S:(k + 1) * S].rearrange("p (t h e) -> p t h e", h=NH1, e=HD1)
                hf = HD1 // 2

                def table(tab, lo, hi):
                    return tab[:, :, lo:hi].rearrange("p t (a e) -> p t a e", a=1).broadcast_to([P, NT, NH1, hi - lo])

                dve.tensor_tensor(a, v, table(cos_s, 0, HD1), ALU.mult)
                dve.tensor_tensor(c[:, :, :, 0:hf], v[:, :, :, hf:HD1], table(sin_s, 0, hf), ALU.mult)
                mark(dve.tensor_tensor(c[:, :, :, hf:HD1], v[:, :, :, 0:hf], table(sin_s, hf, HD1), ALU.mult))
                settle()
                ins = dve.tensor_tensor(v, a, c, ALU.add)
            ins.then_inc(tok_made, 1)

        def maxima(base, odd, n, i, part):
            tile = part // 2
            for k in range(2):
                for j in range(2 * (part % 2), 2 * (part % 2) + 2):
                    dve.wait_ge(ring_filled, base + n + 1)
                    ins = dve.tensor_reduce(mx1[i][:, tile, j, k:k + 1], ring[(odd + n) % RING][:, :], AX_X,
                                            ALU.max).then_inc(ring_freed, 1)
                    n += 1
            if part % 8 == 7:
                dve.wait_ge(ring_freed, base + n)
                ts = slice(part // 8 * TPH, (part // 8 + 1) * TPH)
                q = qs[i][:, ts, :].rearrange("p t (j r) -> p t j r", r=SLOT)[:, :, :, ROWS:ROWS + 1]
                dve.tensor_tensor(q.bitcast(F32R), mx1[i][:, ts, :, 0:1], mx1[i][:, ts, :, 1:2], ALU.max).then_inc(max_made, 1)
            return n

        def divide(t, g, i, base, odd, n, half):
            dve.wait_ge(ring_filled, base + n + 1)
            v = ring[(odd + n) % RING][:, :].rearrange("p (t j r) -> p t j r", j=GROUP, r=SLOT)
            d = rden1[:, half, :, :].rearrange("p t (j a) -> p t j a", a=1)
            mark(dve.reciprocal(d, v[:, :, :, HD1:HD1 + 1]))
            settle()
            out = xn[:, i * NT + half * TPH:i * NT + (half + 1) * TPH, bass.ds(g * (GROUP * HD1), GROUP * HD1)]
            ins = dve.tensor_tensor(out.rearrange("p t (j e) -> p t j e", e=HD1), v[:, :, :, 0:HD1],
                                    d.broadcast_to([P, TPH, GROUP, HD1]), ALU.mult)
            ins.then_inc(ring_freed, 1)
            return ins, n + 1

        def att_step(t, g, gp, i, prep=True):
            base, n = RING_A + PER_RING_A * t, int(first(t))
            for beat in range(16):
                if beat == 1 and not first(t):
                    _, n = divide(t - 1, gp, 1 - i, base, RING_A, n, 1)
                if beat == 9:
                    _, n = divide(t, g, i, base, RING_A, n, 0)
                if prep:
                    n = maxima(base, RING_A, n, 1 - i, beat)
            return base, n

        n = 0
        for part in range(16):
            n = maxima(RING_INIT, RING_INIT, n, 0, part)
        att_step(0, 0, 0, 0)
        chain[:] = [chain[0] + chain[1], 0]
        start, per = chain[0], 2 * 2
        with dve.Fori(0, 3) as it:
            chain[0] = start + per * it
            att_step(2 * it + 1, it, it, 1)
            att_step(2 * it + 2, it + 1, it, 0)
        assert chain[1] == per
        chain[:] = [start + 3 * per, 0]
        base, n = att_step(A_STEPS - 1, NG - 1, NG - 1, 1, prep=False)
        ins, n = divide(A_STEPS - 1, NG - 1, 1, base, base, n, 1)
        n += base

        for q in range(TT // TPH):
            dve.wait_ge(ring_filled, n + 1)
            dve.tensor_copy(xt[:, q * HALF:(q + 1) * HALF], ring[n % RING][:, :]).then_inc(ring_freed, 1)
            n += 1

        dve.wait_ge(ex_made, 1)
        cells = TT * 2 * H2

        def cube(a):
            return a.rearrange("p (c e) -> p c e", e=E2)

        pr = gates[:, :, :].rearrange("p t (c e) -> p (t c) e", e=E2)
        oh1, eq = cube(t_a[:, :]), cube(t_b[:, :])
        oh2 = xn[:, :, :].rearrange("p t (c e) -> p (t c) e", e=E2)
        top = [small[:, k, :].rearrange("p (c a) -> p c a", a=1) for k in range(6)]

        def wide(a):
            return a.broadcast_to([P, cells, E2])

        rank_w = rank_s[:, :].rearrange("p (a e) -> p a e", a=1).broadcast_to([P, cells, E2])

        dve.wait_ge(ring_filled, n)
        then(dve.tensor_scalar(pr, pr, 1.0, None, ALU.add))
        then(dve.reciprocal(pr, pr))
        for k, (src, oh) in enumerate(((pr, oh1), (eq, oh2))):
            then(dve.tensor_reduce(top[k], src, AX_X, ALU.max))
            then(dve.tensor_tensor(oh, src, wide(top[k]), ALU.is_equal))
            then(dve.tensor_tensor(oh, oh, rank_w, ALU.mult))
            then(dve.tensor_reduce(top[2], oh, AX_X, ALU.max))
            then(dve.tensor_tensor(oh, oh, wide(top[2]), ALU.is_equal))
            if k == 0:
                then(dve.scalar_tensor_tensor(out=eq, in0=oh1, scalar=-4.0, in1=pr, op0=ALU.mult, op1=ALU.add))
        then(dve.tensor_tensor(top[3], top[0], top[1], ALU.add))
        then(dve.tensor_scalar(top[3], top[3], 1e-9, None, ALU.max))
        then(dve.reciprocal(top[4], top[3]))
        then(dve.tensor_scalar(top[4], top[4], rs_b[:, 0:1], None, ALU.mult))
        for k in range(2):
            then(dve.tensor_tensor(top[k], top[k], top[4], ALU.mult))
        then(dve.tensor_tensor(oh1, oh1, wide(top[0]), ALU.mult))
        then(dve.tensor_tensor(oh2, oh2, wide(top[1]), ALU.mult))
        then(dve.tensor_tensor(pr, oh1, oh2, ALU.add))

        bias = bo_s[:, :].rearrange("p (a d) -> p a d", a=1)
        then(dve.tensor_tensor(acc[:, :, :], acc[:, :, :], bias.broadcast_to([P, TT, D]), ALU.add))
        for q in range(TT // TPH):
            dve.wait_ge(ring_filled, n + 1)
            part = acc[:, q * TPH:(q + 1) * TPH, :]
            ins = dve.tensor_tensor(part, ring[n % RING][:, :].rearrange("p (t d) -> p t d", d=D), part, ALU.add)
            ins.then_inc(ring_freed, 1)
            n += 1

        def head_gates(h, off, i):
            a = gates[:, i * NT:(i + 1) * NT, bass.ds(h * E2 + off, E2)]
            return a

        def value_gates(h, i):
            mark(dve.tensor_copy(gv[:, :, :], head_gates(h, 0, i)))
            settle()

        def output_gates(s, h, i, half):
            ts = slice(half * TPH, (half + 1) * TPH)
            dve.wait_ge(st_freed, den_fill(s, half) + 1)
            dve.reciprocal(rden[:, ts], den[:, ts]).then_inc(den_used, 1)
            dve.wait_ge(den_used, 2 * s + half + 1)
            g = head_gates(h, H2 * E2, i)[:, ts, :]
            r = rden[:, ts].rearrange("p (t a) -> p t a", a=1)
            mark(dve.tensor_tensor(go[:, ts, :], g, r.broadcast_to([P, TPH, E2]), ALU.mult))
            settle()

        def experts(base, odd, n, beat, i, prep, post):
            both = int(prep and post)
            if post:
                dve.wait_ge(ring_freed, base + n - 2)
            for e in range(2):
                for k in range(4):
                    x = 4 * e + k
                    for turn in range(1 - int(prep), 1 + int(post)):
                        at = n + turn * both
                        if turn:
                            out, g = acc[:, (1 - i) * NT + beat, :], go[:, beat, x:x + 1]
                        else:
                            out, g = v_acc[1 - i][:, beat, :], gv[:, beat, x:x + 1]
                        if k == 0:
                            dve.wait_ge(ring_filled, base + at + 1)
                            if e:
                                dve.wait_ge(ring_freed, base + at - both)
                        else:
                            settle(but=both if k < 3 or turn == 0 else 0)
                        src = ring[(odd + at) % RING][:, k * P:(k + 1) * P]
                        if x == 0 and turn == 0:
                            ins = dve.tensor_scalar(out, src, g, None, ALU.mult)
                        else:
                            ins = dve.scalar_tensor_tensor(out=out, in0=src, scalar=g, in1=out, op0=ALU.mult, op1=ALU.add)
                        if k < 3:
                            mark(ins)
                        else:
                            ins.then_inc(ring_freed, 1)
                n += 1 + both
            return n

        def query_maxima(base, odd, n, i, tile):
            for k in range(2):
                dve.wait_ge(ring_filled, base + n + 1)
                ins = dve.tensor_reduce(mx2[:, tile, k:k + 1], ring[(odd + n) % RING][:, :], AX_X, ALU.max).then_inc(ring_freed, 1)
                n += 1
            if tile % TPH == TPH - 1:
                dve.wait_ge(ring_freed, base + n)
                ts = slice(tile + 1 - TPH, tile + 1)
                m = m2[:, ts].rearrange("p (t a) -> p t a", a=1)
                mark(dve.tensor_tensor(m, mx2[:, ts, 0:1], mx2[:, ts, 1:2], ALU.max))
                settle()
                eye = neg_ident[:, :].rearrange("p (a q) -> p a q", a=1).broadcast_to([P, TPH, P])
                dve.tensor_tensor(diag[i][:, ts, :], eye, m.broadcast_to([P, TPH, P]), ALU.mult).then_inc(diag_made, 1)
            return n

        def step(s, r, h_next, h_last, prep=True):
            i, post = r % 2, not first(s)
            base, n = RING_F + PER_RING_F * s, 16 * int(first(s))
            if prep:
                dve.wait_ge(prob_used, USED_F + 8 * s)
                value_gates(h_next, 1 - i)
            for beat in range(8):
                if post and beat % 4 == 0:
                    output_gates(s - 1, h_last, 1 - i, beat // 4)
                n = experts(base, RING_F, n, beat, i, prep, post)
                if prep:
                    n = query_maxima(base, RING_F, n, 1 - i, beat)
            return base, n

        value_gates(0, 0)
        n = 0
        for beat in range(8):
            n = experts(RING_F - 16, RING_F - 16, n, beat, 1, True, False)
            n = query_maxima(RING_F - 16, RING_F - 16, n, 0, beat)
        step(0, 0, 0, 0)
        step(1, 1, 1, 0)
        chain[:] = [chain[0] + chain[1], 0]
        start, per = chain[0], 4 * (1 + 2 + 8 * 12 + 2)
        with dve.Fori(0, 3) as it:
            chain[0] = start + per * it
            for r in range(2, 6):
                step(4 * it + r, r, 2 * it + (r + 1) // 2, 2 * it + (r - 1) // 2)
        assert chain[1] == per, (chain, per)
        chain[:] = [start + 3 * per, 0]
        for s in range(14, F_STEPS):
            base, n = step(s, s % 4, (s + 1) // 2, (s - 1) // 2, prep=s < F_STEPS - 1)
        last = F_STEPS - 1
        for beat in range(8):
            if beat % 4 == 0:
                output_gates(last, H2 - 1, 1, beat // 4)
            n = experts(base, RING_F, n, beat, 0, False, True)

    ctx.close()


def kernel(L0_attn_x, L0_attn_wq, L0_attn_bq, L0_attn_wk, L0_attn_bk, L0_attn_wv, L0_attn_bv, L0_attn_wo, L0_attn_bo,
           L0_ffn_q_w, L0_ffn_k_w, L0_ffn_v_w, L0_ffn_o_w, L0_ffn_sel_v_w, L0_ffn_sel_o_w, L0_ffn_route_scale):
    import numpy as np
    import concourse.bacc as bacc
    from concourse.bass_utils import run_bass_kernel_spmd

    inv = (np.float32(1.0) / np.float32(10000.0) ** (np.arange(0, HD1, 2, dtype=np.float32) / np.float32(HD1))).astype(np.float32)
    ang = np.arange(S, dtype=np.float32)[:, None] * inv[None, :]
    cos = np.concatenate([np.cos(ang), np.cos(ang)], 1).astype(np.float32)
    sin = np.concatenate([-np.sin(ang), np.sin(ang)], 1).astype(np.float32)
    rank = np.arange(E2, 0, -1).astype(np.float32)
    f = np.asarray
    q_w = f(L0_ffn_q_w).reshape(H2, P, D).transpose(0, 2, 1)
    k_w = f(L0_ffn_k_w).reshape(H2, P, D).transpose(0, 2, 1)
    v_w = f(L0_ffn_v_w).reshape(H2, E2, D, P).transpose(0, 2, 1, 3).reshape(H2, D, E2 * P)
    o_w = f(L0_ffn_o_w).reshape(H2, E2, P, D).transpose(0, 2, 1, 3).reshape(H2, P, E2 * D)
    arrays = {
        "x": f(L0_attn_x),
        "w_in": np.concatenate([f(L0_attn_wq).T, f(L0_attn_wk).T, f(L0_attn_wv).T, f(L0_ffn_sel_v_w).T, f(L0_ffn_sel_o_w).T], 1),
        "wo_t": f(L0_attn_wo).T,
        "b_in": np.concatenate([f(L0_attn_bq), f(L0_attn_bk), f(L0_attn_bv)]),
        "bo": f(L0_attn_bo),
        "rs": f(L0_ffn_route_scale),
        "cos": cos, "sin": sin, "rank": rank,
        "wf": np.concatenate([q_w, k_w, v_w, o_w], 2),
    }
    nc = bacc.Bacc("TRN2", target_bir_lowering=False, num_devices=1)
    feed, args = {}, {}
    for name, a in arrays.items():
        feed[f"in_{name}"] = np.ascontiguousarray(a)
        args[name] = nc.dram_tensor(f"in_{name}", a.shape, F32, kind="ExternalInput").ap()
    args["out"] = nc.dram_tensor("out", (B, S, D), F32, kind="ExternalOutput").ap()
    build(nc, **args)
    return run_bass_kernel_spmd(nc, [feed], core_ids=[0]).results[0]["out"]
```

```python
from contextlib import ExitStack

import concourse.bass as bass
from concourse import mybir

F32 = mybir.dt.float32
F32R = mybir.dt.float32r
ALU = mybir.AluOpType
ACT = mybir.ActivationFunctionType
AX_X = mybir.AxisListType.X

P = 128
B, S, D = 2, 1024, 128
NT = S // P
TT = B * NT
NH1, HD1 = 16, 8
SLOT = 32
GROUP = P // SLOT
NG = NH1 // GROUP
ROWS = 3 * HD1
H2, E2 = 8, 8
HALF = 512
TPH = HALF // P
EPS = 1e-5
SCALE1 = 1.0 / float(HD1) ** 0.5
SCALE2 = 1.0 / float(P) ** 0.5
NP = 4
RING = 3
PADS = 8
WA, WB = 2 * P + E2 * D, E2 * D

RING_INIT = B * 2 + TT
ST_A, ST_A_LAST = 3, 33
RING_A = RING_INIT + 4 * NT * 2 - 1
PER_ST_A, PER_RING_A = 36, 66
A_STEPS, F_STEPS = NG * B, H2 * B
ST_F = ST_A + PER_ST_A * (A_STEPS - 1) + ST_A_LAST + 2 - 1
RING_AO = RING_A + PER_RING_A * (A_STEPS - 1) + 3
RING_1 = RING_AO + 2 * TT // TPH
RING_F = RING_1 + 32 - 16
PER_ST_F, PER_RING_F = 12, 48
PER_SUM = 6
USED_F = A_STEPS * 16


def wait(eng, sem, value):
    if not isinstance(value, int) or value > 0:
        eng.wait_ge(sem, value)


def first(s):
    return isinstance(s, int) and s == 0


def ended(s):
    return isinstance(s, int) and s == F_STEPS - 1


def exp_fill(s, beat):
    prep = 0 if ended(s) else 2
    late = int(first(s)) if beat == 0 else 1
    return ST_F + PER_ST_F * s + prep + late + beat + int(beat > 4)


def den_fill(s, half):
    if half == 0:
        return exp_fill(s, 5) - 1
    return exp_fill(s, 7) + 1 if ended(s) else exp_fill(s + 1, 1) - 1


def prob_at(beat):
    return 2 + beat // 4 if beat % 4 == 0 else beat % 2


def values_freed(s, half):
    if half:
        return RING_F + PER_RING_F * s + 16 * int(first(s))
    if first(s):
        return RING_F - 16 + 3 * 4 + 2
    return RING_F + PER_RING_F * (s - 1) + (16 + 3 * 4 + 2 if isinstance(s, int) and s == 1 else 3 * 6 + 3)


def moved_fill(s, k):
    return ST_F - 1 + k if first(s) else ST_F + PER_ST_F * (s - 1) + k + (1 if isinstance(s, int) and s == 1 else 0)


def queries_fill(t, half):
    if half:
        return ST_A + PER_ST_A * t + (2 if isinstance(t, int) and t == A_STEPS - 1 else 4)
    return 2 if first(t) else ST_A + PER_ST_A * (t - 1) + 21 + 2


def final(s):
    return isinstance(s, int) and s >= F_STEPS - B


def build(nc, x, w_in, wo_t, b_in, bo, rs, cos, sin, rank, wf, out):
    ctx = ExitStack()
    common, early, late = ExitStack(), ExitStack(), ExitStack()

    def sb(stack, name, shape, dt=F32):
        return stack.enter_context(nc.sbuf_tensor(name, shape, dt))

    def sem(name):
        return ctx.enter_context(nc.semaphore(name))

    acc = sb(common, "acc", [P, TT, D])
    x_hi = sb(common, "x_hi", [P, B * S], F32R)
    x_lo = sb(common, "x_lo", [P, B * S], F32R)
    gates = sb(common, "gates", [P, TT, 2 * H2 * E2])
    prob = sb(common, "prob", [P, NP, 2 * HALF])
    p_sum = prob[:, 2:4, :]
    ident = sb(common, "ident", [P, P])
    neg_ident = sb(common, "neg_ident", [P, P])
    ones = sb(common, "ones", [P, P])
    ones_r = sb(common, "ones_r", [P, P], F32R)
    pad = sb(common, "pad", [P, PADS])
    rs_b = sb(common, "rs_b", [P, 1])
    q_t, k_t, qs, ks, v_st = [], [], [], [], []
    for i in range(B):
        q_t.append(sb(early, f"q_t{i}", [P, GROUP, S], F32R))
        k_t.append(sb(early, f"k_t{i}", [P, S], F32R))
        qs.append(sb(early, f"qs{i}", [P, NT, P]))
        ks.append(sb(early, f"ks{i}", [P, NT, P]))
        v_st.append(sb(early, f"v_st{i}", [P, NT, GROUP, SLOT]))
    w_in_s = sb(early, "w_in_s", [P, 4 * P])
    b_in_s = sb(early, "b_in_s", [P, 3 * P])
    xn = sb(early, "xn", [P, TT, D])
    xt = sb(early, "xt", [P, B * S])
    wo_s = sb(early, "wo_s", [P, P])
    bo_s = sb(early, "bo_s", [P, P])
    cos_s = sb(early, "cos_s", [P, NT, HD1])
    sin_s = sb(early, "sin_s", [P, NT, HD1])
    rank_s = sb(early, "rank_s", [P, E2])
    stats = sb(early, "stats", [P, TT, 6])
    mv = sb(early, "mv", [P, TT, 2])
    rstd = sb(early, "rstd", [P, TT])
    newton = sb(early, "newton", [P, TT])
    qk_tok = sb(early, "qk_tok", [P, TT, 2 * P])
    v_tok = sb(early, "v_tok", [P, TT, P])
    t_a = sb(early, "t_a", [P, TT * D])
    t_b = sb(early, "t_b", [P, TT * D])
    small = sb(early, "small", [P, 5, TT * 2 * H2])
    mx1 = [sb(early, f"mx1{i}", [P, NT, GROUP, 2]) for i in range(2)]
    o_t = sb(early, "o_t", [P, 2, HALF])
    rden1 = sb(early, "rden1", [P, 2, TPH, GROUP])
    early.close()
    raw_a = sb(late, "raw_a", [P, WA])
    raw_b = sb(late, "raw_b", [P, WB])
    a_hi, a_lo = [sb(late, "a_hi0", [P, WA], F32R)], [sb(late, "a_lo0", [P, WA], F32R)]
    b_hi, b_lo = [sb(late, "b_hi0", [P, WB], F32R)], [sb(late, "b_lo0", [P, WB], F32R)]
    a_hi.append(sb(late, "a_hi1", [P, WA], F32R))
    qk_f = sb(late, "qk_f", [P, 2, S])
    qk_hi, qk_lo = [sb(late, "qk_hi0", [P, 2, S], F32R)], [sb(late, "qk_lo0", [P, 2, S], F32R)]
    v_acc = sb(late, "v_acc", [P, NT, P])
    diag = [sb(late, "diag0", [P, NT, P], F32R)]
    mx2 = sb(late, "mx2", [P, NT, 2])
    m2 = sb(late, "m2", [P, NT])
    gv = sb(late, "gv", [P, NT, E2])
    go = sb(late, "go", [P, NT, E2])
    den = sb(late, "den", [P, NT])
    rden = sb(late, "rden", [P, NT])
    a_lo.append(sb(late, "a_lo1", [P, WA], F32R))
    b_hi.append(sb(late, "b_hi1", [P, WB], F32R))
    b_lo.append(sb(late, "b_lo1", [P, WB], F32R))
    qk_hi.append(sb(late, "qk_hi1", [P, 2, S], F32R))
    qk_lo.append(sb(late, "qk_lo1", [P, 2, S], F32R))
    v_hi = [sb(late, f"v_hi{i}", [P, NT, P], F32R) for i in range(2)]
    v_lo = [sb(late, f"v_lo{i}", [P, NT, P], F32R) for i in range(2)]
    diag.append(sb(late, "diag1", [P, NT, P], F32R))
    prob_hi = sb(late, "prob_hi", [P, 2, 2 * HALF], F32R)
    prob_lo = sb(late, "prob_lo", [P, 2, 2 * HALF], F32R)
    ctx_f = sb(late, "ctx_f", [P, HALF])
    ctx_hi = sb(late, "ctx_hi", [P, S], F32R)
    ctx_lo = sb(late, "ctx_lo", [P, S], F32R)
    late.close()
    common.close()

    st = [ctx.enter_context(nc.psum_tensor(f"st{i}", [P, 2 * HALF], F32)) for i in range(2)]
    ring = [ctx.enter_context(nc.psum_tensor(f"ring{i}", [P, HALF], F32)) for i in range(RING)]
    pv = ctx.enter_context(nc.psum_tensor("pv", [P, HALF], F32))

    x_loaded, w_loaded = [sem(f"x_loaded{b}") for b in range(B)], sem("w_loaded")
    raw_a_loaded, raw_b_loaded, stored = sem("raw_a_loaded"), sem("raw_b_loaded"), sem("stored")
    consts_made, memset_done = sem("consts_made"), sem("memset_done")
    st_filled, st_freed = sem("st_filled"), sem("st_freed")
    ring_filled, ring_freed = sem("ring_filled"), sem("ring_freed")
    prob_used, prob_summed = sem("prob_used"), sem("prob_summed")
    var_made, sqrt_made = sem("var_made"), sem("sqrt_made")
    xn_made, x_hi_made, x_lo_made = sem("xn_made"), sem("x_hi_made"), sem("x_lo_made")
    tok_made, ex_made = sem("tok_made"), sem("ex_made")
    stack_made, v_stack_made = sem("stack_made"), sem("v_stack_made")
    max_made, o_t_made = sem("max_made"), sem("o_t_made")
    wa_hi_made, wa_split, wb_hi_made, wb_split = sem("wa_hi_made"), sem("wa_split"), sem("wb_hi_made"), sem("wb_split")
    qk_split, diag_made = sem("qk_split"), sem("diag_made")
    ctx_hi_made, ctx_split = sem("ctx_hi_made"), sem("ctx_split")
    prob_total, den_used = sem("prob_total"), sem("den_used")
    prob_split, v_hi_made, v_split = sem("prob_split"), sem("v_hi_made"), sem("v_split")
    pool_step, stack_step, dve_step = sem("pool_step"), sem("stack_step"), sem("dve_step")

    block = ctx.enter_context(nc.Block())

    def tiles(b, half=0):
        t = b * NT + half * TPH
        return slice(t, t + TPH)

    @block.sync
    def _(sp):
        for b in range(B):
            sp.dma_start(acc[:, b * NT:(b + 1) * NT, :], x[b].rearrange("(t p) d -> p t d", p=P)).then_inc(x_loaded[b], 16)
        sp.dma_start(w_in_s[:, :], w_in).then_inc(w_loaded, 16)
        sp.dma_start(b_in_s[:, :], b_in.rearrange("(a n) -> a n", a=1).broadcast_to([P, 3 * P])).then_inc(w_loaded, 16)
        sp.dma_start(cos_s[:, :, :], cos.rearrange("(t p) e -> p t e", p=P)).then_inc(w_loaded, 16)
        sp.dma_start(sin_s[:, :, :], sin.rearrange("(t p) e -> p t e", p=P)).then_inc(w_loaded, 16)
        sp.dma_start(rank_s[:, :], rank.rearrange("(a n) -> a n", a=1).broadcast_to([P, E2])).then_inc(w_loaded, 16)
        sp.dma_start(bo_s[:, :], bo.rearrange("(a n) -> a n", a=1).broadcast_to([P, P])).then_inc(w_loaded, 16)
        sp.dma_start(rs_b[:, :], rs.rearrange("(a n) -> a n", a=1).broadcast_to([P, 1])).then_inc(w_loaded, 16)
        sp.dma_start(wo_s[:, :], wo_t).then_inc(w_loaded, 16)
        sp.wait_ge(prob_used, USED_F - 16)
        sp.dma_start(raw_a[:, :], wf[0, :, 0:WA]).then_inc(raw_a_loaded, 16)
        sp.dma_start(raw_b[:, :], wf[0, :, WA:WA + WB]).then_inc(raw_b_loaded, 16)
        with sp.Fori(1, H2) as h:
            sp.wait_ge(wa_split, h)
            sp.dma_start(raw_a[:, :], wf[bass.ds(h, 1), :, 0:WA].rearrange("a p n -> p (a n)")).then_inc(raw_a_loaded, 16)
            sp.wait_ge(wb_split, h)
            sp.dma_start(raw_b[:, :], wf[bass.ds(h, 1), :, WA:WA + WB].rearrange("a p n -> p (a n)")).then_inc(raw_b_loaded, 16)
        for b in range(B):
            sp.wait_ge(ring_freed, RING_F + PER_RING_F * (F_STEPS - 1) + 16 * (b + 1))
            sp.dma_start(out[b].rearrange("(t p) d -> p t d", p=P), acc[:, b * NT:(b + 1) * NT, :]).then_inc(stored, 16)
        sp.wait_ge(stored, 16 * B)


    @block.gpsimd
    def _(pool):
        links = [0]

        def link(ins):
            links[0] += 1
            ins.then_inc(pool_step, 1)
            pool.wait_ge(pool_step, links[0])

        pads = [0]

        def stand_alone():
            pads[0] = (pads[0] + 1) % PADS
            pool.tensor_tensor(pad[:, pads[0]:pads[0] + 1], ones[:, 0:1], ones[:, 0:1], ALU.mult)

        pool.memset(ones[:, :], 1.0)
        for i in range(2):
            pool.memset(qs[i][:, :, :], 0.0)
            pool.memset(ks[i][:, :, :], 0.0)
            pool.memset(v_st[i][:, :, :, :], 0.0)
            pool.memset(q_t[i][:, :, :].bitcast(F32), 0.0)
        link(pool.memset(ident[:, :], 0.0))
        for i in range(2):
            for j in range(GROUP):
                pool.memset(ks[i][:, :, j * SLOT + ROWS:j * SLOT + ROWS + 1], -1.0)
                pool.memset(v_st[i][:, :, j, HD1:HD1 + 1], 1.0)
        link(pool.affine_select(out=ident[:, :], in_=ident[:, :], compare_op=ALU.not_equal, fill=1.0, base=0,
                                pattern=[[-1, P]], channel_multiplier=1))
        pool.tensor_copy(ones_r[:, :], ones[:, :])
        pool.tensor_scalar(neg_ident[:, :], ident[:, :], -1.0, None, ALU.mult).then_inc(consts_made, 1)

        for n in range(B * 2):
            cols = slice(n * HALF, (n + 1) * HALF)
            pool.wait_ge(x_hi_made, n + 1)
            pool.tensor_tensor(x_lo[:, cols], xt[:, cols], x_hi[:, cols], ALU.subtract).then_inc(x_lo_made, 1)

        def heads(src, b, g, off):
            a = src[:, b * NT:(b + 1) * NT, bass.ds(g * (GROUP * HD1) + off, GROUP * HD1)]
            return a.rearrange("p t (j e) -> p t j e", e=HD1)

        def make_stack(u, g, i):
            if isinstance(u, int) and u < 2:
                pool.wait_ge(tok_made, i + 1)
            else:
                pool.wait_ge(st_freed, ST_A + PER_ST_A * (u - 2) + 5)
                stand_alone()

            def part(buf, k):
                a = buf[:, :, :].rearrange("p t (j r) -> p t j r", r=SLOT)
                return a[:, :, :, k * HD1:(k + 1) * HD1]

            q, k = heads(qk_tok, i, g, 0), heads(qk_tok, i, g, P)
            pool.memset(qs[i][:, :, :].rearrange("p t (j r) -> p t j r", r=SLOT)[:, :, :, ROWS:ROWS + 1], 0.0)
            pool.tensor_copy(part(qs[i], 0).bitcast(F32R), q)
            pool.tensor_copy(part(ks[i], 0).bitcast(F32R), k)
            pool.tensor_copy(part(qs[i], 2).bitcast(F32R), q)
            ins = pool.tensor_copy(part(ks[i], 1).bitcast(F32R), k)
            ins.then_inc(stack_step, 1)
            pool.wait_ge(stack_step, u + 1)
            stand_alone()
            pool.tensor_tensor(part(qs[i], 1).bitcast(F32R), q, part(qs[i], 0), ALU.subtract)
            pool.tensor_tensor(part(ks[i], 2).bitcast(F32R), k, part(ks[i], 0), ALU.subtract).then_inc(stack_made, 1)

        def make_values(u, g, i):
            wait(pool, prob_used, 16 * (u - 1))
            stand_alone()
            pool.tensor_copy(v_st[i][:, :, :, 0:HD1], heads(v_tok, i, g, 0)).then_inc(v_stack_made, 1)

        make_stack(0, 0, 0)
        make_values(0, 0, 0)
        make_stack(1, 0, 1)
        pool.tensor_copy(v_st[1][:, :, :, 0:HD1], heads(v_tok, 1, 0, 0)).then_inc(v_stack_made, 1)
        make_stack(2, 1, 0)
        with pool.Fori(0, 2) as it:
            make_values(2 * it + 2, it + 1, 0)
            make_stack(2 * it + 3, it + 1, 1)
            make_values(2 * it + 3, it + 1, 1)
            make_stack(2 * it + 4, it + 2, 0)
        make_values(6, 3, 0)
        make_stack(7, 3, 1)
        make_values(7, 3, 1)

        def split_a(h, i):
            pool.wait_ge(wa_hi_made, h)
            pool.tensor_tensor(a_lo[i][:, :], raw_a[:, :], a_hi[i][:, :], ALU.subtract).then_inc(wa_split, 1)

        def split_b(h, i):
            pool.wait_ge(wb_hi_made, h)
            pool.tensor_tensor(b_lo[i][:, :], raw_b[:, :], b_hi[i][:, :], ALU.subtract).then_inc(wb_split, 1)

        def split_qk(s, i, k):
            pool.wait_ge(st_freed, moved_fill(s, k) + 1)
            pool.tensor_tensor(qk_lo[i][:, k, :], qk_f[:, k, :], qk_hi[i][:, k, :], ALU.subtract).then_inc(qk_split, 1)

        def split_values(s, i, half):
            ts = slice(half * TPH, (half + 1) * TPH)
            pool.wait_ge(v_hi_made, 2 * s + half + 1)
            pool.tensor_tensor(v_lo[i][:, ts, :], v_acc[:, ts, :], v_hi[i][:, ts, :], ALU.subtract).then_inc(v_split, 1)

        def split_context(s, half):
            cols = slice(half * HALF, (half + 1) * HALF)
            pool.wait_ge(ctx_hi_made, 2 * s + half + 1)
            pool.tensor_tensor(ctx_lo[:, cols], ctx_f[:, :], ctx_hi[:, cols], ALU.subtract).then_inc(ctx_split, 1)

        def step(s, r, h, last=False):
            for beat in range(8):
                half, n = beat // 4, beat % 4
                pool.wait_ge(st_freed, exp_fill(s, beat) + 1)
                p = prob[:, prob_at(beat), :]
                pool.tensor_tensor(prob_lo[:, beat % 2, :], p, prob_hi[:, beat % 2, :], ALU.subtract).then_inc(prob_split, 1)
                if n:
                    wait(pool, prob_summed, PER_SUM * s + 3 * half + n - 1)
                    pool.tensor_tensor(p_sum[:, half, :], p_sum[:, half, :], p, ALU.add).then_inc(prob_summed, 1)
                elif half == 0:
                    if not first(s):
                        split_context(s - 1, 1)
                    split_values(s, r % 2, 1)
                else:
                    split_context(s, 0)
                    if not last:
                        split_values(s + 1, (r + 1) % 2, 0)
                if n == 3:
                    pool.wait_ge(prob_summed, PER_SUM * s + 3 * half + 3)
                    pool.tensor_tensor(p_sum[:, half, 0:HALF], p_sum[:, half, 0:HALF], p_sum[:, half, HALF:],
                                       ALU.add).then_inc(prob_total, 1)
                if beat in (1, 2) and not last:
                    split_qk(s + 1, (r + 1) % 2, beat - 1)
                if beat == 5 and not final(s):
                    (split_b if r % 2 else split_a)(h + 1, (r // 2 + 1) % 2)

        pool.wait_ge(raw_a_loaded, 16)
        link(pool.tensor_copy(a_hi[0][:, :], raw_a[:, :]))
        pool.tensor_tensor(a_lo[0][:, :], raw_a[:, :], a_hi[0][:, :], ALU.subtract).then_inc(wa_split, 1)
        pool.wait_ge(raw_b_loaded, 16)
        link(pool.tensor_copy(b_hi[0][:, :], raw_b[:, :]))
        pool.tensor_tensor(b_lo[0][:, :], raw_b[:, :], b_hi[0][:, :], ALU.subtract).then_inc(wb_split, 1)
        split_qk(0, 0, 0)
        split_qk(0, 0, 1)
        pool.wait_ge(ring_freed, RING_1)
        split_values(0, 0, 0)
        step(0, 0, 0)
        step(1, 1, 0)
        with pool.Fori(0, 3) as it:
            for r in range(2, 6):
                step(4 * it + r, r, 2 * it + r // 2)
        for s in range(14, F_STEPS):
            step(s, s % 4, s // 2, last=s == F_STEPS - 1)
        split_context(F_STEPS - 1, 1)

    @block.scalar
    def _(act):
        for b in range(B):
            act.wait_ge(var_made, b + 1)
            ts = slice(b * NT, (b + 1) * NT)
            act.activation(rstd[:, ts], mv[:, ts, 1:2].rearrange("p t a -> p (t a)"), ACT.Sqrt).then_inc(sqrt_made, 1)
        for n in range(B * 2):
            cols = slice(n * HALF, (n + 1) * HALF)
            act.wait_ge(ring_freed, n // 2 * (2 + NT) + n % 2 + 1)
            act.activation(x_hi[:, cols], xt[:, cols], ACT.Copy).then_inc(x_hi_made, 1)
        act.wait_ge(tok_made, B)
        act.activation(gates[:, :, :], gates[:, :, :], ACT.Exp, scale=-1.0).then_inc(ex_made, 1)

        def move_heads(bank, i, cols):
            for j in range(GROUP):
                rows = slice(j * SLOT, (j + 1) * SLOT)
                ins = act.activation(q_t[i][rows, j, cols], bank[rows, 0:cols.stop - cols.start], ACT.Copy)
            ins.then_inc(st_freed, 1)

        def move_stacks(base, odd, n, i):
            act.wait_ge(st_filled, base + n + 1)
            act.activation(k_t[i][:, :], st[(odd + n) % 2][:, :], ACT.Copy).then_inc(st_freed, 1)
            act.wait_ge(st_filled, base + n + 2)
            move_heads(st[(odd + n + 1) % 2], i, slice(0, S))

        def move_queries(base, odd, n, i, half):
            act.wait_ge(st_filled, base + n + 1)
            move_heads(st[(odd + n) % 2], i, slice(half * HALF, (half + 1) * HALF))

        def att_step(t, i, prep=True):
            base, n = ST_A + PER_ST_A * t, 0
            if prep:
                move_stacks(base, ST_A, n, 1 - i)
                n += 2
            for beat in range(16):
                if beat == 1:
                    move_queries(base, ST_A, n, i, 1)
                    n += 1
                if beat == 9 and prep:
                    move_queries(base, ST_A, n, 1 - i, 0)
                    n += 1
                wait(act, prob_used, 16 * t + beat - 1)
                for pair in range(2):
                    act.wait_ge(st_filled, base + n + 1)
                    act.activation(prob[:, 2 * (beat % 2) + pair, :], st[(ST_A + n) % 2][:, :], ACT.Exp,
                                   scale=SCALE1).then_inc(st_freed, 1)
                    n += 1
                if beat % 8 == 7:
                    half = beat // 8
                    act.wait_ge(prob_used, 16 * t + 8 * half + 8)
                    act.activation(o_t[:, half, :], pv[:, :], ACT.Copy).then_inc(o_t_made, 1)

        move_stacks(0, 0, 0, 0)
        move_queries(0, 0, 2, 0, 0)
        att_step(0, 0)
        with act.Fori(0, 3) as it:
            att_step(2 * it + 1, 1)
            att_step(2 * it + 2, 0)
        att_step(A_STEPS - 1, 1, prep=False)


        def head_a(h, i):
            act.wait_ge(raw_a_loaded, 16 * h + 16)
            act.activation(a_hi[i][:, :], raw_a[:, :], ACT.Copy).then_inc(wa_hi_made, 1)

        def head_b(h, i):
            act.wait_ge(raw_b_loaded, 16 * h + 16)
            act.activation(b_hi[i][:, :], raw_b[:, :], ACT.Copy).then_inc(wb_hi_made, 1)

        def move_qk(s, i, base, odd, n):
            for k in range(2):
                act.wait_ge(st_filled, base + n + k + 1)
                wait(act, qk_split, 2 * s + k - 1)
                act.activation(qk_f[:, k, :], st[(odd + n + k) % 2][:, :], ACT.Copy)
                act.activation(qk_hi[i][:, k, :], st[(odd + n + k) % 2][:, :],
                               ACT.Copy).then_inc(st_freed, 1)

        def move_den(s, half, base, n):
            act.wait_ge(st_filled, base + n + 1)
            wait(act, den_used, 2 * s - 1 + half)
            act.activation(den[:, half * TPH:(half + 1) * TPH], st[(ST_F + n) % 2][:, 0:TPH],
                           ACT.Copy).then_inc(st_freed, 1)

        def move_context(s, half):
            act.wait_ge(prob_used, USED_F + 8 * s + 4 * half + 4)
            wait(act, ctx_split, 2 * s + half)
            act.activation(ctx_f[:, :], pv[:, :], ACT.Copy)
            act.activation(ctx_hi[:, half * HALF:(half + 1) * HALF], pv[:, :], ACT.Copy).then_inc(ctx_hi_made, 1)

        def head_values(s, i, half):
            act.wait_ge(ring_freed, values_freed(s, half))
            ts = slice(half * TPH, (half + 1) * TPH)
            act.activation(v_hi[i][:, ts, :], v_acc[:, ts, :], ACT.Copy).then_inc(v_hi_made, 1)

        def step(s, r, h, last=False):
            i = r % 2
            base, n = ST_F + PER_ST_F * s, int(first(s))
            if not last:
                move_qk(s + 1, 1 - i, base, ST_F, n)
                n += 2
            for beat in range(8):
                if beat == 1 and not first(s):
                    move_den(s - 1, 1, base, n)
                    n += 1
                if beat == 5:
                    move_den(s, 0, base, n)
                    n += 1
                act.wait_ge(prob_used, USED_F + (8 * s + beat - 1 if beat or not first(s) else 0))
                if beat % 4:
                    wait(act, prob_summed, PER_SUM * s + 3 * (beat // 4) + (0, 0, -1, 1)[beat % 4])
                act.wait_ge(st_filled, base + n + 1)
                bank = st[(ST_F + n) % 2]
                act.activation(prob_hi[:, beat % 2, :], bank[:, :], ACT.Exp, scale=SCALE2)
                act.activation(prob[:, prob_at(beat), :], bank[:, :], ACT.Exp, scale=SCALE2).then_inc(st_freed, 1)
                n += 1
                if beat == 0:
                    if not first(s):
                        move_context(s - 1, 1)
                    head_values(s, i, 1)
                if beat == 4:
                    move_context(s, 0)
                    if not last:
                        head_values(s + 1, 1 - i, 0)
                if beat == 1 and not final(s):
                    (head_b if r % 2 else head_a)(h + 1, (r // 2 + 1) % 2)
            return n

        move_qk(0, 0, ST_F - 1, ST_F - 1, 0)
        act.wait_ge(ring_freed, RING_1)
        head_values(0, 0, 0)
        step(0, 0, 0)
        step(1, 1, 0)
        with act.Fori(0, 3) as it:
            for r in range(2, 6):
                step(4 * it + r, r, 2 * it + r // 2)
        for s in range(14, F_STEPS):
            n = step(s, s % 4, s // 2, last=s == F_STEPS - 1)
        move_context(F_STEPS - 1, 1)
        move_den(F_STEPS - 1, 1, ST_F + PER_ST_F * (F_STEPS - 1), n)

    @block.tensor
    def _(pe):
        pe.wait_ge(consts_made, 1)
        n = 0
        for b in range(B):
            for half in range(2):
                pe.wait_ge(xn_made, 2 * b + half + 1)
                wait(pe, ring_freed, n - 2)
                for c in range(TPH):
                    ins = pe.transpose(ring[n % RING][:, c * P:(c + 1) * P], xn[:, b * NT + half * TPH + c, :], ident[:, :])
                ins.then_inc(ring_filled, 1)
                n += 1
            if b == 0:
                pe.wait_ge(w_loaded, 16 * 8)
            for t in range(b * NT, (b + 1) * NT):
                pe.wait_ge(ring_freed, b * (2 + NT) + t % NT // TPH + 1)
                wait(pe, ring_freed, n - 2)
                pe.matmul(ring[n % RING][:, :], xt[:, t * P:(t + 1) * P], w_in_s[:, :],
                          start=True, stop=True).then_inc(ring_filled, 1)
                n += 1

        def product(out, l_hi, l_lo, r_hi, r_lo, begin=True, more=False):
            pe.matmul(out, l_hi, r_hi, start=begin, stop=False)
            pe.matmul(out, l_lo, r_hi, start=False, stop=False)
            return pe.matmul(out, l_hi, r_lo, start=False, stop=not more)

        def project(s, i, hp, base, odd, n):
            for k in range(2):
                pe.wait_ge(st_freed, base + n + k - 1)
                w = slice((1 - k) * P, (2 - k) * P)
                for half in range(2):
                    cols = slice(i * S + half * HALF, i * S + (half + 1) * HALF)
                    ins = product(st[(odd + n + k) % 2][:, half * HALF:(half + 1) * HALF], a_hi[hp][:, w], a_lo[hp][:, w],
                                  x_hi[:, cols], x_lo[:, cols])
                ins.then_inc(st_filled, 1)

        def turn_stacks(u, base, odd, n, i):
            pe.wait_ge(stack_made, u + 1)
            for k, buf in enumerate((ks[i], qs[i])):
                wait(pe, st_freed, base + n + k - 1)
                for c in range(NT):
                    ins = pe.transpose(st[(odd + n + k) % 2][:, c * P:(c + 1) * P], buf[:, c, :], ident[:, :])
                ins.then_inc(st_filled, 1)

        def turn_queries(u, base, odd, n, i, half):
            pe.wait_ge(max_made, 2 * u + half + 1)
            pe.wait_ge(st_freed, base + n - 1)
            for c in range(TPH):
                ins = pe.transpose(st[(odd + n) % 2][:, c * P:(c + 1) * P], qs[i][:, half * TPH + c, :], ident[:, :])
            ins.then_inc(st_filled, 1)

        def query_scores(base, odd, n, i, part, q):
            tile, k, j = part // 2, q // 2, 2 * (part % 2) + q % 2
            wait(pe, ring_freed, base + n - 2)
            pe.matmul(ring[(odd + n) % RING][:, :], q_t[i][:, j, tile * P:(tile + 1) * P],
                      k_t[i][:, k * HALF:(k + 1) * HALF], start=True, stop=True).then_inc(ring_filled, 1)
            return n + 1

        def turn_output(t, base, odd, n, half):
            pe.wait_ge(o_t_made, 2 * t + half + 1)
            pe.wait_ge(ring_freed, base + n - 2)
            for c in range(TPH):
                ins = pe.transpose(ring[(odd + n) % RING][:, c * P:(c + 1) * P], o_t[:, half, c * P:(c + 1) * P], ident[:, :])
            ins.then_inc(ring_filled, 1)
            return n + 1

        def att_values(t, i, beat, made):
            half, kt = beat // 8, beat % 8
            if kt == 0:
                wait(pe, o_t_made, 2 * t + half)
                pe.wait_ge(v_stack_made, t + 1)
            pe.wait_ge(st_freed, made)
            for j in range(GROUP):
                ins = pe.matmul(pv[j * SLOT:(j + 1) * SLOT, :], v_st[i][:, kt, j, :],
                                prob[:, 2 * (beat % 2) + j // 2, (j % 2) * HALF:(j % 2 + 1) * HALF],
                                start=kt == 0, stop=kt == NT - 1)
            ins.then_inc(prob_used, 1)

        def att_step(t, i, prep=True):
            sb_, s_n = ST_A + PER_ST_A * t, 0
            rb, r_n = RING_A + PER_RING_A * t, int(first(t))
            if prep:
                turn_stacks(t + 1, sb_, ST_A, s_n, 1 - i)
                s_n += 2
            for beat in range(16):
                half, kt = beat // 8, beat % 8
                if beat == 1:
                    turn_queries(t, sb_, ST_A, s_n, i, 1)
                    s_n += 1
                    if not first(t):
                        r_n = turn_output(t - 1, rb, RING_A, r_n, 1)
                if beat == 9:
                    if prep:
                        turn_queries(t + 1, sb_, ST_A, s_n, 1 - i, 0)
                        s_n += 1
                    r_n = turn_output(t, rb, RING_A, r_n, 0)
                if kt == 0:
                    pe.wait_ge(st_freed, queries_fill(t, half) + 1)
                if prep and beat == 0:
                    pe.wait_ge(st_freed, sb_ + 2)
                for j in range(GROUP):
                    if j % 2 == 0:
                        pe.wait_ge(st_freed, sb_ + s_n - 1)
                    ins = pe.matmul(st[(ST_A + s_n) % 2][:, (j % 2) * HALF:(j % 2 + 1) * HALF],
                                    k_t[i][:, kt * P:(kt + 1) * P], q_t[i][:, j, half * HALF:(half + 1) * HALF],
                                    start=True, stop=True)
                    if j % 2:
                        ins.then_inc(st_filled, 1)
                        s_n += 1
                    if prep and j:
                        r_n = query_scores(rb, RING_A, r_n, 1 - i, beat, j - 1)
                if beat:
                    att_values(t, i, beat - 1, made)
                if prep:
                    r_n = query_scores(rb, RING_A, r_n, 1 - i, beat, 3)
                made = sb_ + s_n
            att_values(t, i, 15, made)
            return rb, r_n

        turn_stacks(0, 0, 0, 0, 0)
        pe.wait_ge(st_freed, 2)
        n = 0
        for part in range(16):
            for q in range(4):
                n = query_scores(RING_INIT, RING_INIT, n, 0, part, q)
            if part == 7:
                turn_queries(0, 0, 0, 2, 0, 0)
        att_step(0, 0)
        with pe.Fori(0, 3) as it:
            att_step(2 * it + 1, 1)
            att_step(2 * it + 2, 0)
        rb, n = att_step(A_STEPS - 1, 1, prep=False)
        n = rb + turn_output(A_STEPS - 1, rb, rb, n, 1)

        pe.wait_ge(wa_split, 1)
        project(0, 0, 0, ST_F - 1, ST_F - 1, 0)

        for q in range(TT // TPH):
            if q == 0:
                pe.wait_ge(ring_freed, RING_AO)
            pe.wait_ge(ring_freed, n - 2)
            for c in range(TPH):
                ins = pe.transpose(ring[n % RING][:, c * P:(c + 1) * P], xn[:, q * TPH + c, :], ident[:, :])
            ins.then_inc(ring_filled, 1)
            n += 1
        for q in range(TT // TPH):
            pe.wait_ge(ring_freed, RING_AO + q + 1)
            pe.wait_ge(ring_freed, n - 2)
            for c in range(TPH):
                t = q * TPH + c
                ins = pe.matmul(ring[n % RING][:, c * P:(c + 1) * P], xt[:, t * P:(t + 1) * P], wo_s[:, :],
                                start=True, stop=True)
            ins.then_inc(ring_filled, 1)
            n += 1
        assert n == RING_1

        def experts(base, odd, n, l_hi, l_lo, tile, r_hi, r_lo, half):
            rows = slice(tile * P, (tile + 1) * P)
            pe.wait_ge(ring_freed, base + n - 2)
            product(ring[(odd + n) % RING][:, :], l_hi[:, rows], l_lo[:, rows], r_hi[:, half], r_lo[:, half]).then_inc(ring_filled, 1)
            return n + 1

        def values(base, odd, n, i, hp, beat, e):
            half = slice(2 * P + e * HALF, 2 * P + (e + 1) * HALF)
            return experts(base, odd, n, x_hi, x_lo, i * NT + beat, a_hi[hp], a_lo[hp], half)

        def outputs(base, odd, n, hp, beat, e):
            return experts(base, odd, n, ctx_hi, ctx_lo, beat, b_hi[hp], b_lo[hp], slice(e * HALF, (e + 1) * HALF))

        def maxima(base, odd, n, i, tile, k):
            pe.wait_ge(ring_freed, base + n - 2)
            pe.matmul(ring[(odd + n) % RING][:, :], qk_hi[i][:, 1, tile * P:(tile + 1) * P],
                      qk_hi[i][:, 0, k * HALF:(k + 1) * HALF], start=True, stop=True).then_inc(ring_filled, 1)
            return n + 1

        def denominators(s, half, base, odd, n):
            pe.wait_ge(prob_total, 2 * s + half + 1)
            pe.wait_ge(st_freed, base + n - 1)
            for c in range(TPH):
                ins = pe.matmul(st[(odd + n) % 2][:, c:c + 1], p_sum[:, half, c * P:(c + 1) * P], ones[:, 0:1],
                                start=True, stop=True)
            ins.then_inc(st_filled, 1)
            return n + 1

        def att_products(s, i, beat):
            half, n = beat // 4, beat % 4
            if n == 0:
                if first(s) and half == 0:
                    pe.wait_ge(o_t_made, 2 * A_STEPS)
                else:
                    pe.wait_ge(ctx_hi_made, 2 * s + half)
            if half == 0 and n % 2 == 0:
                pe.wait_ge(v_split, 2 * s + n // 2 + 1)
            pe.wait_ge(prob_split, 8 * s + beat + 1)
            for k in range(2):
                kt, cols = 2 * n + k, slice(k * HALF, (k + 1) * HALF)
                ins = product(pv[:, :], v_hi[i][:, kt, :], v_lo[i][:, kt, :], prob_hi[:, beat % 2, cols],
                              prob_lo[:, beat % 2, cols], begin=kt == 0, more=kt < NT - 1)
            ins.then_inc(prob_used, 1)

        def step(s, r, h, prep=True):
            i, post = r % 2, not first(s)
            nh, ph = (r + 1) // 2 % 2, (r - 1) // 2 % 2
            sb_, s_n = ST_F + PER_ST_F * s, int(first(s))
            rb, r_n = RING_F + PER_RING_F * s, 16 * int(first(s))
            if prep:
                if i:
                    pe.wait_ge(wa_split, h + 2)
                project(s + 1, 1 - i, nh, sb_, ST_F, s_n)
                s_n += 2
            for beat in range(8):
                half, n = beat // 4, beat % 4
                if beat == 1 and post:
                    s_n = denominators(s - 1, 1, sb_, ST_F, s_n)
                if beat == 5:
                    s_n = denominators(s, 0, sb_, ST_F, s_n)
                if post and n == 0:
                    if i == 1 and half == 0:
                        pe.wait_ge(wb_split, h + 1)
                    pe.wait_ge(ctx_split, 2 * s - 1 + half)
                if prep:
                    r_n = values(rb, RING_F, r_n, 1 - i, nh, beat, 0)
                if post:
                    r_n = outputs(rb, RING_F, r_n, ph, beat, 0)
                if prep:
                    r_n = values(rb, RING_F, r_n, 1 - i, nh, beat, 1)
                if beat == 0:
                    pe.wait_ge(qk_split, 2 * s + 2)
                if n == 0:
                    pe.wait_ge(diag_made, 2 * s + half + 1)
                pe.wait_ge(st_freed, sb_ + s_n - 1)
                cols = slice(half * HALF, (half + 1) * HALF)
                for k in range(2):
                    rows = slice((2 * n + k) * P, (2 * n + k + 1) * P)
                    out = st[(ST_F + s_n) % 2][:, k * HALF:(k + 1) * HALF]
                    product(out, qk_hi[i][:, 0, rows], qk_lo[i][:, 0, rows], qk_hi[i][:, 1, cols], qk_lo[i][:, 1, cols], more=True)
                    ins = pe.matmul(out, ones_r[:, :], diag[i][:, half * TPH:(half + 1) * TPH, :], start=False, stop=True)
                    if k == 0 and post:
                        r_n = outputs(rb, RING_F, r_n, ph, beat, 1)
                ins.then_inc(st_filled, 1)
                s_n += 1
                if prep:
                    if beat == 0:
                        pe.wait_ge(st_freed, moved_fill(s + 1, 1) + 1)
                    r_n = maxima(rb, RING_F, r_n, 1 - i, beat, 0)
                if beat:
                    att_products(s, i, beat - 1)
                elif post:
                    att_products(s - 1, 1 - i, 7)
                if prep:
                    r_n = maxima(rb, RING_F, r_n, 1 - i, beat, 1)
            return sb_, s_n, rb, r_n

        pe.wait_ge(st_freed, moved_fill(0, 1) + 1)
        n = 0
        for beat in range(8):
            for e in range(2):
                n = values(RING_1, RING_1, n, 0, 0, beat, e)
            for k in range(2):
                n = maxima(RING_1, RING_1, n, 0, beat, k)
        step(0, 0, 0)
        step(1, 1, 0)
        with pe.Fori(0, 3) as it:
            for r in range(2, 6):
                step(4 * it + r, r, 2 * it + r // 2)
        for s in range(14, F_STEPS):
            sb_, s_n, rb, r_n = step(s, s % 4, s // 2, prep=s < F_STEPS - 1)
        att_products(F_STEPS - 1, (F_STEPS - 1) % 2, 7)
        denominators(F_STEPS - 1, 1, sb_, ST_F, s_n)
        for beat in range(8):
            if beat % 4 == 0:
                pe.wait_ge(ctx_split, 2 * (F_STEPS - 1) + beat // 4 + 1)
            for e in range(2):
                r_n = outputs(rb, RING_F, r_n, (H2 - 1) % 2, beat, e)

    @block.vector
    def _(dve):
        chain = [0, 0]

        def mark(ins):
            chain[1] += 1
            return ins.then_inc(dve_step, 1)

        def settle(but=0):
            dve.wait_ge(dve_step, chain[0] + chain[1] - but)

        def then(ins):
            mark(ins)
            settle()

        n = 0
        for b in range(B):
            dve.wait_ge(x_loaded[b], 16)
            ts = slice(b * NT, (b + 1) * NT)
            for t in range(b * NT, (b + 1) * NT):
                ins = dve.bn_stats(stats[:, t, :], acc[:, t, :])
            mark(ins)
            settle()
            for t in range(b * NT, (b + 1) * NT):
                ins = dve.bn_aggr(mv[:, t, :], stats[:, t, :])
            mark(ins)
            settle()
            var = mv[:, ts, 1:2].rearrange("p t a -> p (t a)")
            dve.tensor_scalar(var, var, EPS, None, ALU.add).then_inc(var_made, 1)
            dve.wait_ge(sqrt_made, b + 1)
            r, z = rstd[:, ts], newton[:, ts]
            then(dve.reciprocal(r, r))
            then(dve.tensor_tensor(z, r, r, ALU.mult))
            then(dve.tensor_tensor(z, z, var, ALU.mult))
            then(dve.tensor_scalar(z, z, -0.5, 1.5, ALU.mult, ALU.add))
            then(dve.tensor_tensor(r, r, z, ALU.mult))
            for t in range(b * NT, (b + 1) * NT):
                ins = dve.tensor_scalar(xn[:, t, :], acc[:, t, :], mv[:, t, 0:1], rstd[:, t:t + 1], ALU.subtract, ALU.mult)
                if t % TPH == TPH - 1:
                    ins.then_inc(xn_made, 1)
            for half in range(2):
                dve.wait_ge(ring_filled, n + 1)
                cols = slice(b * S + half * HALF, b * S + (half + 1) * HALF)
                dve.tensor_copy(xt[:, cols], ring[n % RING][:, :]).then_inc(ring_freed, 1)
                n += 1
            if b == 0:
                dve.wait_ge(w_loaded, 16 * 8)
            for t in range(b * NT, (b + 1) * NT):
                dve.wait_ge(ring_filled, n + 1)
                bank = ring[n % RING]
                dve.tensor_tensor(qk_tok[:, t, :], bank[:, 0:2 * P], b_in_s[:, 0:2 * P], ALU.add)
                dve.tensor_tensor(v_tok[:, t, :], bank[:, 2 * P:3 * P], b_in_s[:, 2 * P:3 * P], ALU.add)
                dve.tensor_copy(gates[:, t, :], bank[:, 3 * P:4 * P]).then_inc(ring_freed, 1)
                n += 1
            dve.wait_ge(ring_freed, n)
            for k in range(2):
                v = qk_tok[:, ts, k * P:(k + 1) * P].rearrange("p t (h e) -> p t h e", e=HD1)
                a = t_a[:, k * S:(k + 1) * S].rearrange("p (t h e) -> p t h e", h=NH1, e=HD1)
                c = t_b[:, k * S:(k + 1) * S].rearrange("p (t h e) -> p t h e", h=NH1, e=HD1)
                hf = HD1 // 2

                def table(tab, lo, hi):
                    return tab[:, :, lo:hi].rearrange("p t (a e) -> p t a e", a=1).broadcast_to([P, NT, NH1, hi - lo])

                dve.tensor_tensor(a, v, table(cos_s, 0, HD1), ALU.mult)
                dve.tensor_tensor(c[:, :, :, 0:hf], v[:, :, :, hf:HD1], table(sin_s, 0, hf), ALU.mult)
                mark(dve.tensor_tensor(c[:, :, :, hf:HD1], v[:, :, :, 0:hf], table(sin_s, hf, HD1), ALU.mult))
                settle()
                ins = dve.tensor_tensor(v, a, c, ALU.add)
            ins.then_inc(tok_made, 1)

        def maxima(base, odd, n, i, part):
            tile = part // 2
            for k in range(2):
                for j in range(2 * (part % 2), 2 * (part % 2) + 2):
                    dve.wait_ge(ring_filled, base + n + 1)
                    ins = dve.tensor_reduce(mx1[i][:, tile, j, k:k + 1], ring[(odd + n) % RING][:, :], AX_X,
                                            ALU.max).then_inc(ring_freed, 1)
                    n += 1
            if part % 8 == 7:
                dve.wait_ge(ring_freed, base + n)
                ts = slice(part // 8 * TPH, (part // 8 + 1) * TPH)
                q = qs[i][:, ts, :].rearrange("p t (j r) -> p t j r", r=SLOT)[:, :, :, ROWS:ROWS + 1]
                dve.tensor_tensor(q.bitcast(F32R), mx1[i][:, ts, :, 0:1], mx1[i][:, ts, :, 1:2], ALU.max).then_inc(max_made, 1)
            return n

        def divide(t, g, i, base, odd, n, half):
            dve.wait_ge(ring_filled, base + n + 1)
            v = ring[(odd + n) % RING][:, :].rearrange("p (t j r) -> p t j r", j=GROUP, r=SLOT)
            d = rden1[:, half, :, :].rearrange("p t (j a) -> p t j a", a=1)
            mark(dve.reciprocal(d, v[:, :, :, HD1:HD1 + 1]))
            settle()
            out = xn[:, i * NT + half * TPH:i * NT + (half + 1) * TPH, bass.ds(g * (GROUP * HD1), GROUP * HD1)]
            ins = dve.tensor_tensor(out.rearrange("p t (j e) -> p t j e", e=HD1), v[:, :, :, 0:HD1],
                                    d.broadcast_to([P, TPH, GROUP, HD1]), ALU.mult)
            ins.then_inc(ring_freed, 1)
            return ins, n + 1

        def att_step(t, g, gp, i, prep=True):
            base, n = RING_A + PER_RING_A * t, int(first(t))
            for beat in range(16):
                if beat == 1 and not first(t):
                    _, n = divide(t - 1, gp, 1 - i, base, RING_A, n, 1)
                if beat == 9:
                    _, n = divide(t, g, i, base, RING_A, n, 0)
                if prep:
                    n = maxima(base, RING_A, n, 1 - i, beat)
            return base, n

        def gate():
            dve.wait_ge(ex_made, 1)
            cells = TT * 2 * H2

            def cube(a):
                return a.rearrange("p (c e) -> p c e", e=E2)

            pr = gates[:, :, :].rearrange("p t (c e) -> p (t c) e", e=E2)
            oh1, eq = cube(t_a[:, :]), cube(t_b[:, :])
            oh2 = cube(qk_tok[:, 0:NT, :].rearrange("p t n -> p (t n)"))
            top = [small[:, k, :].rearrange("p (c a) -> p c a", a=1) for k in range(5)]

            def wide(a):
                return a.broadcast_to([P, cells, E2])

            rank_w = rank_s[:, :].rearrange("p (a e) -> p a e", a=1).broadcast_to([P, cells, E2])

            dve.wait_ge(stack_made, A_STEPS)
            then(dve.tensor_scalar(pr, pr, 1.0, None, ALU.add))
            then(dve.reciprocal(pr, pr))
            for k, (src, oh) in enumerate(((pr, oh1), (eq, oh2))):
                then(dve.tensor_reduce(top[k], src, AX_X, ALU.max))
                then(dve.tensor_tensor(oh, src, wide(top[k]), ALU.is_equal))
                then(dve.tensor_tensor(oh, oh, rank_w, ALU.mult))
                then(dve.tensor_reduce(top[2], oh, AX_X, ALU.max))
                then(dve.tensor_tensor(oh, oh, wide(top[2]), ALU.is_equal))
                if k == 0:
                    then(dve.scalar_tensor_tensor(out=eq, in0=oh1, scalar=-4.0, in1=pr, op0=ALU.mult, op1=ALU.add))
            then(dve.tensor_tensor(top[3], top[0], top[1], ALU.add))
            then(dve.tensor_scalar(top[3], top[3], 1e-9, None, ALU.max))
            then(dve.reciprocal(top[4], top[3]))
            then(dve.tensor_scalar(top[4], top[4], rs_b[:, 0:1], None, ALU.mult))
            for k in range(2):
                then(dve.tensor_tensor(top[k], top[k], top[4], ALU.mult))
            then(dve.tensor_tensor(oh1, oh1, wide(top[0]), ALU.mult))
            then(dve.tensor_tensor(oh2, oh2, wide(top[1]), ALU.mult))
            then(dve.tensor_tensor(pr, oh1, oh2, ALU.add))

            bias = bo_s[:, :].rearrange("p (a d) -> p a d", a=1)
            then(dve.tensor_tensor(acc[:, :, :], acc[:, :, :], bias.broadcast_to([P, TT, D]), ALU.add))

        n = 0
        for part in range(16):
            n = maxima(RING_INIT, RING_INIT, n, 0, part)
        att_step(0, 0, 0, 0)
        chain[:] = [chain[0] + chain[1], 0]
        start, per = chain[0], 2 * 2
        with dve.Fori(0, 3) as it:
            chain[0] = start + per * it
            att_step(2 * it + 1, it, it, 1)
            att_step(2 * it + 2, it + 1, it, 0)
        assert chain[1] == per
        chain[:] = [start + 3 * per, 0]
        last, n = A_STEPS - 1, 0
        base = RING_A + PER_RING_A * last
        _, n = divide(last - 1, NG - 1, 0, base, base, n, 1)
        gate()
        for half in range(2):
            _, n = divide(last, NG - 1, 1, base, base, n, half)
        n += base

        for q in range(TT // TPH):
            dve.wait_ge(ring_filled, n + 1)
            dve.tensor_copy(xt[:, q * HALF:(q + 1) * HALF], ring[n % RING][:, :]).then_inc(ring_freed, 1)
            n += 1

        for q in range(TT // TPH):
            dve.wait_ge(ring_filled, n + 1)
            part = acc[:, q * TPH:(q + 1) * TPH, :]
            ins = dve.tensor_tensor(part, ring[n % RING][:, :].rearrange("p (t d) -> p t d", d=D), part, ALU.add)
            ins.then_inc(ring_freed, 1)
            n += 1

        def head_gates(h, off, i):
            a = gates[:, i * NT:(i + 1) * NT, bass.ds(h * E2 + off, E2)]
            return a

        def value_gates(h, i):
            mark(dve.tensor_copy(gv[:, :, :], head_gates(h, 0, i)))
            settle()

        def output_gates(s, h, i, half):
            ts = slice(half * TPH, (half + 1) * TPH)
            dve.wait_ge(st_freed, den_fill(s, half) + 1)
            dve.reciprocal(rden[:, ts], den[:, ts]).then_inc(den_used, 1)
            dve.wait_ge(den_used, 2 * s + half + 1)
            g = head_gates(h, H2 * E2, i)[:, ts, :]
            r = rden[:, ts].rearrange("p (t a) -> p t a", a=1)
            mark(dve.tensor_tensor(go[:, ts, :], g, r.broadcast_to([P, TPH, E2]), ALU.mult))
            settle()

        def experts(base, odd, n, beat, i, made, prep, post):
            both = int(prep and post)
            if prep and beat % 4 == 0:
                wait(dve, v_split, 2 * made + beat // 4 - 1)
            if post:
                dve.wait_ge(ring_freed, base + n - 2)
            both_turns = ((0, 0), (0, 1), (1, 0), (0, 2), (1, 1), (0, 3), (1, 2), (1, 3))
            for e in range(2):
                marks, last = 0, [0, 0]
                for turn, k in (both_turns if both else [(int(post), k) for k in range(4)]):
                    x, at = 4 * e + k, n + turn * both
                    if turn:
                        out, g = acc[:, (1 - i) * NT + beat, :], go[:, beat, x:x + 1]
                    else:
                        out, g = v_acc[:, beat, :], gv[:, beat, x:x + 1]
                    if k == 0:
                        dve.wait_ge(ring_filled, base + at + 1)
                        if e:
                            dve.wait_ge(ring_freed, base + at - both)
                    else:
                        settle(but=marks - last[turn])
                    src = ring[(odd + at) % RING][:, k * P:(k + 1) * P]
                    if x == 0 and turn == 0:
                        ins = dve.tensor_scalar(out, src, g, None, ALU.mult)
                    else:
                        ins = dve.scalar_tensor_tensor(out=out, in0=src, scalar=g, in1=out, op0=ALU.mult, op1=ALU.add)
                    if k < 3:
                        mark(ins)
                        marks += 1
                        last[turn] = marks
                    else:
                        ins.then_inc(ring_freed, 1)
                n += 1 + both
            return n

        def query_maxima(base, odd, n, i, tile):
            for k in range(2):
                dve.wait_ge(ring_filled, base + n + 1)
                ins = dve.tensor_reduce(mx2[:, tile, k:k + 1], ring[(odd + n) % RING][:, :], AX_X, ALU.max).then_inc(ring_freed, 1)
                n += 1
            if tile % TPH == TPH - 1:
                dve.wait_ge(ring_freed, base + n)
                ts = slice(tile + 1 - TPH, tile + 1)
                m = m2[:, ts].rearrange("p (t a) -> p t a", a=1)
                mark(dve.tensor_tensor(m, mx2[:, ts, 0:1], mx2[:, ts, 1:2], ALU.max))
                settle()
                eye = neg_ident[:, :].rearrange("p (a q) -> p a q", a=1).broadcast_to([P, TPH, P])
                dve.tensor_tensor(diag[i][:, ts, :], eye, m.broadcast_to([P, TPH, P]), ALU.mult).then_inc(diag_made, 1)
            return n

        def step(s, r, h_next, h_last, prep=True):
            i, post = r % 2, not first(s)
            base, n = RING_F + PER_RING_F * s, 16 * int(first(s))
            if prep:
                value_gates(h_next, 1 - i)
            for beat in range(8):
                if post and beat % 4 == 0:
                    output_gates(s - 1, h_last, 1 - i, beat // 4)
                n = experts(base, RING_F, n, beat, i, s + 1, prep, post)
                if prep:
                    n = query_maxima(base, RING_F, n, 1 - i, beat)
            return base, n

        value_gates(0, 0)
        n = 0
        for beat in range(8):
            n = experts(RING_F - 16, RING_F - 16, n, beat, 1, 0, True, False)
            n = query_maxima(RING_F - 16, RING_F - 16, n, 0, beat)
        step(0, 0, 0, 0)
        step(1, 1, 1, 0)
        chain[:] = [chain[0] + chain[1], 0]
        start, per = chain[0], 4 * (1 + 2 + 8 * 12 + 2)
        with dve.Fori(0, 3) as it:
            chain[0] = start + per * it
            for r in range(2, 6):
                step(4 * it + r, r, 2 * it + (r + 1) // 2, 2 * it + (r - 1) // 2)
        assert chain[1] == per, (chain, per)
        chain[:] = [start + 3 * per, 0]
        for s in range(14, F_STEPS):
            base, n = step(s, s % 4, (s + 1) // 2, (s - 1) // 2, prep=s < F_STEPS - 1)
        last = F_STEPS - 1
        for beat in range(8):
            if beat % 4 == 0:
                output_gates(last, H2 - 1, 1, beat // 4)
            n = experts(base, RING_F, n, beat, 0, None, False, True)

    ctx.close()


def kernel(L0_attn_x, L0_attn_wq, L0_attn_bq, L0_attn_wk, L0_attn_bk, L0_attn_wv, L0_attn_bv, L0_attn_wo, L0_attn_bo,
           L0_ffn_q_w, L0_ffn_k_w, L0_ffn_v_w, L0_ffn_o_w, L0_ffn_sel_v_w, L0_ffn_sel_o_w, L0_ffn_route_scale):
    import numpy as np
    import concourse.bacc as bacc
    from concourse.bass_utils import run_bass_kernel_spmd

    inv = (np.float32(1.0) / np.float32(10000.0) ** (np.arange(0, HD1, 2, dtype=np.float32) / np.float32(HD1))).astype(np.float32)
    ang = np.arange(S, dtype=np.float32)[:, None] * inv[None, :]
    cos = np.concatenate([np.cos(ang), np.cos(ang)], 1).astype(np.float32)
    sin = np.concatenate([-np.sin(ang), np.sin(ang)], 1).astype(np.float32)
    rank = np.arange(E2, 0, -1).astype(np.float32)
    f = np.asarray
    q_w = f(L0_ffn_q_w).reshape(H2, P, D).transpose(0, 2, 1)
    k_w = f(L0_ffn_k_w).reshape(H2, P, D).transpose(0, 2, 1)
    v_w = f(L0_ffn_v_w).reshape(H2, E2, D, P).transpose(0, 2, 1, 3).reshape(H2, D, E2 * P)
    o_w = f(L0_ffn_o_w).reshape(H2, E2, P, D).transpose(0, 2, 1, 3).reshape(H2, P, E2 * D)
    arrays = {
        "x": f(L0_attn_x),
        "w_in": np.concatenate([f(L0_attn_wq).T, f(L0_attn_wk).T, f(L0_attn_wv).T, f(L0_ffn_sel_v_w).T, f(L0_ffn_sel_o_w).T], 1),
        "wo_t": f(L0_attn_wo).T,
        "b_in": np.concatenate([f(L0_attn_bq), f(L0_attn_bk), f(L0_attn_bv)]),
        "bo": f(L0_attn_bo),
        "rs": f(L0_ffn_route_scale),
        "cos": cos, "sin": sin, "rank": rank,
        "wf": np.concatenate([q_w, k_w, v_w, o_w], 2),
    }
    nc = bacc.Bacc("TRN2", target_bir_lowering=False, num_devices=1)
    feed, args = {}, {}
    for name, a in arrays.items():
        feed[f"in_{name}"] = np.ascontiguousarray(a)
        args[name] = nc.dram_tensor(f"in_{name}", a.shape, F32, kind="ExternalInput").ap()
    args["out"] = nc.dram_tensor("out", (B, S, D), F32, kind="ExternalOutput").ap()
    build(nc, **args)
    return run_bass_kernel_spmd(nc, [feed], core_ids=[0]).results[0]["out"]
```

```python
from contextlib import ExitStack

import concourse.bass as bass
from concourse import mybir

F32 = mybir.dt.float32
F32R = mybir.dt.float32r
ALU = mybir.AluOpType
ACT = mybir.ActivationFunctionType
AX_X = mybir.AxisListType.X

P = 128
B, S, D = 2, 1024, 128
NT = S // P
TT = B * NT
NH1, HD1 = 16, 8
SLOT = 32
GROUP = P // SLOT
NG = NH1 // GROUP
ROWS = 3 * HD1
H2, E2 = 8, 8
HALF = 512
TPH = HALF // P
EPS = 1e-5
SCALE1 = 1.0 / float(HD1) ** 0.5
SCALE2 = 1.0 / float(P) ** 0.5
NP = 4
RING = 3
PADS = 8
WA, WB = 2 * P + E2 * D, E2 * D

PER_ST_INIT = 1 + NT // 2
ST_INIT = B * PER_ST_INIT
ST_A, ST_A_LAST = ST_INIT + 3, 33
RING_A = 4 * NT * 2 - 1
PER_ST_A, PER_RING_A = 36, 66
A_STEPS, F_STEPS = NG * B, H2 * B
ST_F = ST_A + PER_ST_A * (A_STEPS - 1) + ST_A_LAST + 2 - 1
RING_AO = RING_A + PER_RING_A * (A_STEPS - 1) + 3
RING_1 = RING_AO + 2 * TT // TPH
RING_F = RING_1 + 32 - 16
PER_ST_F, PER_RING_F = 12, 48
PER_SUM = 6
USED_F = A_STEPS * 16


def wait(eng, sem, value):
    if not isinstance(value, int) or value > 0:
        eng.wait_ge(sem, value)


def first(s):
    return isinstance(s, int) and s == 0


def ended(s):
    return isinstance(s, int) and s == F_STEPS - 1


def exp_fill(s, beat):
    prep = 0 if ended(s) else 2
    late = int(first(s)) if beat == 0 else 1
    return ST_F + PER_ST_F * s + prep + late + beat + int(beat > 4)


def den_fill(s, half):
    if half == 0:
        return exp_fill(s, 5) - 1
    return exp_fill(s, 7) + 1 if ended(s) else exp_fill(s + 1, 1) - 1


def prob_at(beat):
    return 2 + beat // 4 if beat % 4 == 0 else beat % 2


def values_freed(s, half):
    if half:
        return RING_F + PER_RING_F * s + 16 * int(first(s))
    if first(s):
        return RING_F - 16 + 8 + 4
    return RING_F + PER_RING_F * (s - 1) + (16 + 3 * 4 + 2 if isinstance(s, int) and s == 1 else 3 * 6 + 3)


def moved_fill(s, k):
    return ST_F - 1 + k if first(s) else ST_F + PER_ST_F * (s - 1) + k + (1 if isinstance(s, int) and s == 1 else 0)


def stack_fill(t):
    return ST_INIT + 1 if first(t) else ST_A + PER_ST_A * (t - 1) + 1


def queries_fill(t, half):
    if half:
        return ST_A + PER_ST_A * t + (8 if isinstance(t, int) and t == A_STEPS - 1 else 10)
    return ST_INIT + 2 if first(t) else ST_A + PER_ST_A * (t - 1) + 25


def final(s):
    return isinstance(s, int) and s >= F_STEPS - B


def build(nc, x, w_in, wo_t, b_in, bo, rs, cos, sin, rank, wf, out):
    ctx = ExitStack()
    common, early, late = ExitStack(), ExitStack(), ExitStack()

    def sb(stack, name, shape, dt=F32):
        return stack.enter_context(nc.sbuf_tensor(name, shape, dt))

    def sem(name):
        return ctx.enter_context(nc.semaphore(name))

    acc = sb(common, "acc", [P, TT, D])
    x_hi = sb(common, "x_hi", [P, B * S], F32R)
    x_lo = sb(common, "x_lo", [P, B * S], F32R)
    gates = sb(common, "gates", [P, TT, 2 * H2 * E2])
    prob = sb(common, "prob", [P, NP, 2 * HALF])
    p_sum = prob[:, 2:4, :]
    ident = sb(common, "ident", [P, P])
    neg_ident = sb(common, "neg_ident", [P, P])
    ones = sb(common, "ones", [P, P])
    ones_r = sb(common, "ones_r", [P, P], F32R)
    pad = sb(common, "pad", [P, PADS])
    head_mask = sb(common, "head_mask", [P, GROUP])
    rs_b = sb(common, "rs_b", [P, 1])
    q_t, k_t, qs, ks, v_st = [], [], [], [], []
    for i in range(B):
        q_t.append(sb(early, f"q_t{i}", [P, GROUP, S], F32R))
        k_t.append(sb(early, f"k_t{i}", [P, S], F32R))
        qs.append(sb(early, f"qs{i}", [P, NT, P]))
        ks.append(sb(early, f"ks{i}", [P, NT, P]))
        v_st.append(sb(early, f"v_st{i}", [P, NT, GROUP, SLOT]))
    w_in_s = sb(early, "w_in_s", [P, 4 * P])
    b_in_s = sb(early, "b_in_s", [P, 3 * P])
    xn = sb(early, "xn", [P, TT, D])
    xt = sb(early, "xt", [P, B * S])
    wo_s = sb(early, "wo_s", [P, P])
    bo_s = sb(early, "bo_s", [P, P])
    cos_s = sb(early, "cos_s", [P, NT, HD1])
    sin_s = sb(early, "sin_s", [P, NT, HD1])
    rank_s = sb(early, "rank_s", [P, E2])
    stats = sb(early, "stats", [P, TT, 6])
    mv = sb(early, "mv", [P, TT, 2])
    rstd = sb(early, "rstd", [P, TT])
    newton = sb(early, "newton", [P, TT])
    qk_tok = sb(early, "qk_tok", [P, TT, 2 * P])
    v_tok = sb(early, "v_tok", [P, TT, P])
    t_a = sb(early, "t_a", [P, TT * D])
    t_b = sb(early, "t_b", [P, TT * D])
    small = sb(early, "small", [P, 5, TT * 2 * H2])
    q_turned = sb(early, "q_turned", [P, S + HALF])
    mx1 = [sb(early, f"mx1{i}", [P, NT, GROUP, 2]) for i in range(2)]
    o_t = sb(early, "o_t", [P, 2, HALF])
    rden1 = sb(early, "rden1", [P, 2, TPH, GROUP])
    early.close()
    raw_a = sb(late, "raw_a", [P, WA])
    raw_b = sb(late, "raw_b", [P, WB])
    a_hi, a_lo = [sb(late, "a_hi0", [P, WA], F32R)], [sb(late, "a_lo0", [P, WA], F32R)]
    b_hi, b_lo = [sb(late, "b_hi0", [P, WB], F32R)], [sb(late, "b_lo0", [P, WB], F32R)]
    a_hi.append(sb(late, "a_hi1", [P, WA], F32R))
    form_f = sb(late, "form_f", [P, P])
    form_hi = sb(late, "form_hi", [P, P], F32R)
    form_lo = sb(late, "form_lo", [P, P], F32R)
    q_f = sb(late, "q_f", [P, S])
    q_hi, q_lo = [sb(late, "q_hi0", [P, S], F32R)], [sb(late, "q_lo0", [P, S], F32R)]
    v_acc = sb(late, "v_acc", [P, NT, P])
    diag = [sb(late, "diag0", [P, NT, P], F32R)]
    mx2 = sb(late, "mx2", [P, NT, 2])
    m2 = sb(late, "m2", [P, NT])
    gv = sb(late, "gv", [P, NT, E2])
    go = sb(late, "go", [P, NT, E2])
    den = sb(late, "den", [P, NT])
    rden = sb(late, "rden", [P, NT])
    a_lo.append(sb(late, "a_lo1", [P, WA], F32R))
    b_hi.append(sb(late, "b_hi1", [P, WB], F32R))
    b_lo.append(sb(late, "b_lo1", [P, WB], F32R))
    q_hi.append(sb(late, "q_hi1", [P, S], F32R))
    q_lo.append(sb(late, "q_lo1", [P, S], F32R))
    v_hi = [sb(late, f"v_hi{i}", [P, NT, P], F32R) for i in range(2)]
    v_lo = [sb(late, f"v_lo{i}", [P, NT, P], F32R) for i in range(2)]
    diag.append(sb(late, "diag1", [P, NT, P], F32R))
    prob_hi = sb(late, "prob_hi", [P, 2, 2 * HALF], F32R)
    prob_lo = sb(late, "prob_lo", [P, 2, 2 * HALF], F32R)
    ctx_f = sb(late, "ctx_f", [P, HALF])
    ctx_hi = sb(late, "ctx_hi", [P, S], F32R)
    ctx_lo = sb(late, "ctx_lo", [P, S], F32R)
    late.close()
    common.close()

    st = [ctx.enter_context(nc.psum_tensor(f"st{i}", [P, 2 * HALF], F32)) for i in range(2)]
    ring = [ctx.enter_context(nc.psum_tensor(f"ring{i}", [P, HALF], F32)) for i in range(RING)]
    pv = ctx.enter_context(nc.psum_tensor("pv", [P, HALF], F32))

    x_loaded, w_loaded = [sem(f"x_loaded{b}") for b in range(B)], sem("w_loaded")
    raw_a_loaded, raw_b_loaded, stored = sem("raw_a_loaded"), sem("raw_b_loaded"), sem("stored")
    consts_made, mask_made = sem("consts_made"), sem("mask_made")
    neg_made = sem("neg_made")
    bias_added, weights_made, gates_made = sem("bias_added"), sem("weights_made"), sem("gates_made")
    st_filled, st_freed = sem("st_filled"), sem("st_freed")
    ring_filled, ring_freed = sem("ring_filled"), sem("ring_freed")
    prob_used, prob_summed = sem("prob_used"), sem("prob_summed")
    var_made, sqrt_made = sem("var_made"), sem("sqrt_made")
    xn_made, x_hi_made, x_lo_made = sem("xn_made"), sem("x_hi_made"), sem("x_lo_made")
    tok_made, ex_made = sem("tok_made"), sem("ex_made")
    stack_made, v_stack_made = sem("stack_made"), sem("v_stack_made")
    max_made, o_t_made = sem("max_made"), sem("o_t_made")
    heads_spread, q_spread = sem("heads_spread"), sem("q_spread")
    wa_hi_made, wa_split, wb_hi_made, wb_split = sem("wa_hi_made"), sem("wa_split"), sem("wb_hi_made"), sem("wb_split")
    form_split, q_split = sem("form_split"), sem("q_split")
    m2_made, diag_made = sem("m2_made"), sem("diag_made")
    ctx_hi_made, ctx_split = sem("ctx_hi_made"), sem("ctx_split")
    prob_total, den_used = sem("prob_total"), sem("den_used")
    prob_split, v_hi_made, v_split = sem("prob_split"), sem("v_hi_made"), sem("v_split")
    pool_step, stack_step, dve_step = sem("pool_step"), sem("stack_step"), sem("dve_step")

    block = ctx.enter_context(nc.Block())

    def tiles(b, half=0):
        t = b * NT + half * TPH
        return slice(t, t + TPH)

    @block.sync
    def _(sp):
        for b in range(B):
            sp.dma_start(acc[:, b * NT:(b + 1) * NT, :], x[b].rearrange("(t p) d -> p t d", p=P)).then_inc(x_loaded[b], 16)
        sp.dma_start(w_in_s[:, :], w_in).then_inc(w_loaded, 16)
        sp.dma_start(b_in_s[:, :], b_in.rearrange("(a n) -> a n", a=1).broadcast_to([P, 3 * P])).then_inc(w_loaded, 16)
        sp.dma_start(cos_s[:, :, :], cos.rearrange("(t p) e -> p t e", p=P)).then_inc(w_loaded, 16)
        sp.dma_start(sin_s[:, :, :], sin.rearrange("(t p) e -> p t e", p=P)).then_inc(w_loaded, 16)
        sp.dma_start(rank_s[:, :], rank.rearrange("(a n) -> a n", a=1).broadcast_to([P, E2])).then_inc(w_loaded, 16)
        sp.dma_start(bo_s[:, :], bo.rearrange("(a n) -> a n", a=1).broadcast_to([P, P])).then_inc(w_loaded, 16)
        sp.dma_start(rs_b[:, :], rs.rearrange("(a n) -> a n", a=1).broadcast_to([P, 1])).then_inc(w_loaded, 16)
        sp.dma_start(wo_s[:, :], wo_t).then_inc(w_loaded, 16)
        sp.wait_ge(prob_used, USED_F - 16)
        sp.dma_start(raw_a[:, :], wf[0, :, 0:WA]).then_inc(raw_a_loaded, 16)
        sp.dma_start(raw_b[:, :], wf[0, :, WA:WA + WB]).then_inc(raw_b_loaded, 16)
        with sp.Fori(1, H2) as h:
            sp.wait_ge(wa_split, h)
            sp.dma_start(raw_a[:, :], wf[bass.ds(h, 1), :, 0:WA].rearrange("a p n -> p (a n)")).then_inc(raw_a_loaded, 16)
            sp.wait_ge(wb_split, h)
            sp.dma_start(raw_b[:, :], wf[bass.ds(h, 1), :, WA:WA + WB].rearrange("a p n -> p (a n)")).then_inc(raw_b_loaded, 16)
        for b, t, fills in ((0, slice(0, NT), 20), (1, slice(0, TPH), 24), (1, slice(TPH, NT), 32)):
            sp.wait_ge(ring_freed, RING_F + PER_RING_F * (F_STEPS - 1) + fills)
            sp.dma_start(out[b].rearrange("(t p) d -> p t d", p=P)[:, t, :],
                         acc[:, b * NT + t.start:b * NT + t.stop, :]).then_inc(stored, 16)
        sp.wait_ge(stored, 16 * 3)


    @block.gpsimd
    def _(pool):
        links = [0]

        def link(ins):
            links[0] += 1
            ins.then_inc(pool_step, 1)
            pool.wait_ge(pool_step, links[0])

        pads = [0]

        def stand_alone():
            pads[0] = (pads[0] + 1) % PADS
            pool.tensor_tensor(pad[:, pads[0]:pads[0] + 1], ones[:, 0:1], ones[:, 0:1], ALU.mult)

        pool.memset(ones[:, :], 1.0)
        for i in range(2):
            pool.memset(qs[i][:, :, :], 0.0)
            pool.memset(ks[i][:, :, :], 0.0)
            pool.memset(v_st[i][:, :, :, :], 0.0)
        link(pool.memset(ident[:, :], 0.0))
        for i in range(2):
            for j in range(GROUP):
                pool.memset(ks[i][:, :, j * SLOT + ROWS:j * SLOT + ROWS + 1], -1.0)
                pool.memset(v_st[i][:, :, j, HD1:HD1 + 1], 1.0)
        link(pool.affine_select(out=ident[:, :], in_=ident[:, :], compare_op=ALU.not_equal, fill=1.0, base=0,
                                pattern=[[-1, P]], channel_multiplier=1))
        pool.tensor_copy(ones_r[:, :], ones[:, :])
        pool.tensor_scalar(neg_ident[:, :], ident[:, :], -1.0, None, ALU.mult).then_inc(consts_made, 1)

        def heads(src, b, g, off):
            a = src[:, b * NT:(b + 1) * NT, bass.ds(g * (GROUP * HD1) + off, GROUP * HD1)]
            return a.rearrange("p t (j e) -> p t j e", e=HD1)

        def make_stack(u, g, i):
            if isinstance(u, int) and u < 2:
                pool.wait_ge(tok_made, i + 1)

            def part(buf, k):
                a = buf[:, :, :].rearrange("p t (j r) -> p t j r", r=SLOT)
                return a[:, :, :, k * HD1:(k + 1) * HD1]

            q, k = heads(qk_tok, i, g, 0), heads(qk_tok, i, g, P)
            pool.memset(qs[i][:, :, :].rearrange("p t (j r) -> p t j r", r=SLOT)[:, :, :, ROWS:ROWS + 1], 0.0)
            pool.tensor_copy(part(qs[i], 0).bitcast(F32R), q)
            pool.tensor_copy(part(ks[i], 0).bitcast(F32R), k)
            pool.tensor_copy(part(qs[i], 2).bitcast(F32R), q)
            ins = pool.tensor_copy(part(ks[i], 1).bitcast(F32R), k)
            ins.then_inc(stack_step, 1)
            pool.wait_ge(stack_step, u + 1)
            stand_alone()
            pool.tensor_tensor(part(qs[i], 1).bitcast(F32R), q, part(qs[i], 0), ALU.subtract)
            pool.tensor_tensor(part(ks[i], 2).bitcast(F32R), k, part(ks[i], 0), ALU.subtract).then_inc(stack_made, 1)

        def make_values(u, g, i):
            if not isinstance(u, int) or u > 1:
                pool.wait_ge(prob_used, 16 * (u - 1))
                stand_alone()
            bias = b_in_s[:, bass.ds(g * (GROUP * HD1) + 2 * P, GROUP * HD1)]
            bias = bias.rearrange("p (a j e) -> p a j e", a=1, e=HD1).broadcast_to([P, NT, GROUP, HD1])
            pool.tensor_tensor(v_st[i][:, :, :, 0:HD1], heads(v_tok, i, g, 0), bias, ALU.add).then_inc(v_stack_made, 1)

        def spread(i, src, cols, heads):
            shape = [P, heads.stop - heads.start, cols.stop - cols.start]
            queries = q_turned[:, src].rearrange("p (a n) -> p a n", a=1).broadcast_to(shape)
            own = head_mask[:, heads].rearrange("p (j a) -> p j a", a=1).broadcast_to(shape)
            pool.tensor_tensor(q_t[i][:, heads, cols], queries, own, ALU.mult).then_inc(q_spread, 1)

        def spread_stack(t, i):
            pool.wait_ge(st_freed, stack_fill(t) + 1)
            spread(i, slice(0, S), slice(0, S), slice(GROUP - 1, GROUP))

        def spread_queries(t, i, half):
            pool.wait_ge(st_freed, queries_fill(t, half) + 1)
            spread(i, slice(S, S + HALF), slice(half * HALF, (half + 1) * HALF), slice(0, GROUP))

        def att_step(t, g_values, g_stack, i, prep=True, stack=True):
            if prep:
                spread_stack(t + 1, 1 - i)
                make_values(t + 1, g_values, 1 - i)
            spread_queries(t, i, 1)
            if stack:
                make_stack(t + 2, g_stack, i)
            if prep:
                spread_queries(t + 1, 1 - i, 0)

        make_stack(0, 0, 0)
        pool.wait_ge(mask_made, 1)
        spread_stack(0, 0)
        make_values(0, 0, 0)
        make_stack(1, 0, 1)
        pool.wait_ge(ex_made, 1)
        pool.tensor_scalar(gates[:, :, :], gates[:, :, :], -1.0, -1.0, ALU.mult, ALU.add).then_inc(neg_made, 1)
        for b in range(B):
            cols = slice(b * S, (b + 1) * S)
            pool.wait_ge(x_hi_made, b + 1)
            pool.tensor_tensor(x_lo[:, cols], xt[:, cols], x_hi[:, cols], ALU.subtract).then_inc(x_lo_made, 1)
        spread_queries(0, 0, 0)
        att_step(0, 0, 1, 0)
        with pool.Fori(0, 2) as it:
            att_step(2 * it + 1, it + 1, it + 1, 1)
            att_step(2 * it + 2, it + 1, it + 2, 0)
        att_step(5, 3, 3, 1)
        att_step(6, 3, None, 0, stack=False)
        att_step(7, None, None, 1, prep=False, stack=False)
        bias = bo_s[:, :].rearrange("p (a d) -> p a d", a=1).broadcast_to([P, TT, D])
        pool.tensor_tensor(acc[:, :, :], acc[:, :, :], bias, ALU.add).then_inc(bias_added, 1)

        def split_a(h, i):
            pool.wait_ge(wa_hi_made, h)
            pool.tensor_tensor(a_lo[i][:, :], raw_a[:, :], a_hi[i][:, :], ALU.subtract).then_inc(wa_split, 1)

        def split_b(h, i):
            pool.wait_ge(wb_hi_made, h)
            pool.tensor_tensor(b_lo[i][:, :], raw_b[:, :], b_hi[i][:, :], ALU.subtract).then_inc(wb_split, 1)

        def split_queries(s, i):
            pool.wait_ge(st_freed, moved_fill(s, 1) + 1)
            pool.tensor_tensor(q_lo[i][:, :], q_f[:, :], q_hi[i][:, :], ALU.subtract).then_inc(q_split, 1)

        def split_values(s, i, half):
            ts = slice(half * TPH, (half + 1) * TPH)
            pool.wait_ge(v_hi_made, 2 * s + half + 1)
            pool.tensor_tensor(v_lo[i][:, ts, :], v_acc[:, ts, :], v_hi[i][:, ts, :], ALU.subtract).then_inc(v_split, 1)

        def split_context(s, half):
            cols = slice(half * HALF, (half + 1) * HALF)
            pool.wait_ge(ctx_hi_made, 2 * s + half + 1)
            pool.tensor_tensor(ctx_lo[:, cols], ctx_f[:, :], ctx_hi[:, cols], ALU.subtract).then_inc(ctx_split, 1)

        def step(s, r, h, last=False):
            for beat in range(8):
                half, n = beat // 4, beat % 4
                pool.wait_ge(st_freed, exp_fill(s, beat) + 1)
                p = prob[:, prob_at(beat), :]
                pool.tensor_tensor(prob_lo[:, beat % 2, :], p, prob_hi[:, beat % 2, :], ALU.subtract).then_inc(prob_split, 1)
                if n:
                    wait(pool, prob_summed, PER_SUM * s + 3 * half + n - 1)
                    pool.tensor_tensor(p_sum[:, half, :], p_sum[:, half, :], p, ALU.add).then_inc(prob_summed, 1)
                elif half == 0:
                    if not first(s):
                        split_context(s - 1, 1)
                    split_values(s, r % 2, 1)
                else:
                    split_context(s, 0)
                    if not last:
                        split_values(s + 1, (r + 1) % 2, 0)
                if n == 3:
                    pool.wait_ge(prob_summed, PER_SUM * s + 3 * half + 3)
                    pool.tensor_tensor(p_sum[:, half, 0:HALF], p_sum[:, half, 0:HALF], p_sum[:, half, HALF:],
                                       ALU.add).then_inc(prob_total, 1)
                if beat == 1 and not last:
                    split_queries(s + 1, (r + 1) % 2)
                if beat == 5 and not final(s):
                    (split_b if r % 2 else split_a)(h + 1, (r // 2 + 1) % 2)

        pool.wait_ge(raw_a_loaded, 16)
        link(pool.tensor_copy(a_hi[0][:, :], raw_a[:, :]))
        pool.tensor_tensor(a_lo[0][:, :], raw_a[:, :], a_hi[0][:, :], ALU.subtract).then_inc(wa_split, 1)
        pool.wait_ge(raw_b_loaded, 16)
        link(pool.tensor_copy(b_hi[0][:, :], raw_b[:, :]))
        pool.tensor_tensor(b_lo[0][:, :], raw_b[:, :], b_hi[0][:, :], ALU.subtract).then_inc(wb_split, 1)
        first_expert = t_a[:, :].rearrange("p (c e) -> p c e", e=E2)
        weight = small[:, 0, :].rearrange("p (c a) -> p c a", a=1).broadcast_to([P, TT * 2 * H2, E2])
        pool.wait_ge(weights_made, 1)
        pool.tensor_tensor(first_expert, first_expert, weight, ALU.mult).then_inc(gates_made, 1)
        split_queries(0, 0)
        pool.wait_ge(ring_freed, RING_1)
        split_values(0, 0, 0)
        step(0, 0, 0)
        step(1, 1, 0)
        with pool.Fori(0, 3) as it:
            for r in range(2, 6):
                step(4 * it + r, r, 2 * it + r // 2)
        for s in range(14, F_STEPS):
            step(s, s % 4, s // 2, last=s == F_STEPS - 1)
        split_context(F_STEPS - 1, 1)

    @block.scalar
    def _(act):
        def root(b):
            act.wait_ge(var_made, b + 1)
            ts = slice(b * NT, (b + 1) * NT)
            act.activation(rstd[:, ts], mv[:, ts, 1:2].rearrange("p t a -> p (t a)"), ACT.Sqrt).then_inc(sqrt_made, 1)

        root(0)
        n = 0
        for b in range(B):
            act.wait_ge(st_filled, n + 1)
            act.activation(xt[:, b * S:(b + 1) * S], st[n % 2][:, :], ACT.Copy).then_inc(st_freed, 1)
            n += 1
            if b + 1 < B:
                root(b + 1)
            for t in range(b * NT, (b + 1) * NT, 2):
                act.wait_ge(st_filled, n + 1)
                bank = st[n % 2][:, :].rearrange("p (t n) -> p t n", n=HALF)
                act.activation(qk_tok[:, t:t + 2, :], bank[:, :, 0:2 * P], ACT.Copy)
                act.activation(v_tok[:, t:t + 2, :], bank[:, :, 2 * P:3 * P], ACT.Copy)
                act.activation(gates[:, t:t + 2, :], bank[:, :, 3 * P:4 * P], ACT.Copy).then_inc(st_freed, 1)
                n += 1
        act.wait_ge(st_freed, n)
        for b in range(B):
            cols = slice(b * S, (b + 1) * S)
            act.activation(x_hi[:, cols], xt[:, cols], ACT.Copy).then_inc(x_hi_made, 1)
        act.activation(gates[:, :, :], gates[:, :, :], ACT.Exp, scale=-1.0).then_inc(ex_made, 1)

        def move_keys(base, odd, n, i):
            act.wait_ge(st_filled, base + n + 1)
            act.activation(k_t[i][:, :], st[(odd + n) % 2][:, :], ACT.Copy).then_inc(st_freed, 1)

        def move_queries(base, odd, n, spreads, maxima=False):
            act.wait_ge(st_filled, base + n + 1)
            wait(act, q_spread, spreads)
            cols = slice(S, S + HALF) if maxima else slice(0, S)
            act.activation(q_turned[:, cols], st[(odd + n) % 2][:, 0:cols.stop - cols.start], ACT.Copy).then_inc(st_freed, 1)

        def move_output(t, half):
            act.wait_ge(prob_used, 16 * t + 8 * half + 8)
            act.activation(o_t[:, half, :], pv[:, :], ACT.Copy).then_inc(o_t_made, 1)

        def att_step(t, i, prep=True):
            base, n = ST_A + PER_ST_A * t, 0
            if prep:
                move_keys(base, ST_A, n, 1 - i)
                move_queries(base, ST_A, n + 1, 3 * t + 2)
                n += 2
            for beat in range(16):
                if beat == 4:
                    move_queries(base, ST_A, n, 3 * t + 2, maxima=True)
                    n += 1
                if beat == 11 and prep:
                    move_queries(base, ST_A, n, 3 * t + 4, maxima=True)
                    n += 1
                wait(act, prob_used, 16 * t + beat - 1)
                for pair in range(2):
                    act.wait_ge(st_filled, base + n + 1)
                    act.activation(prob[:, 2 * (beat % 2) + pair, :], st[(ST_A + n) % 2][:, :], ACT.Exp,
                                   scale=SCALE1).then_inc(st_freed, 1)
                    n += 1
                if beat == 0 and not first(t):
                    move_output(t - 1, 1)
                if beat == 8:
                    move_output(t, 0)

        move_keys(ST_INIT, ST_INIT, 0, 0)
        move_queries(ST_INIT, ST_INIT, 1, 0)
        move_queries(ST_INIT, ST_INIT, 2, 0, maxima=True)
        att_step(0, 0)
        with act.Fori(0, 3) as it:
            att_step(2 * it + 1, 1)
            att_step(2 * it + 2, 0)
        att_step(A_STEPS - 1, 1, prep=False)
        move_output(A_STEPS - 1, 1)


        def head_a(h, i):
            act.wait_ge(raw_a_loaded, 16 * h + 16)
            act.activation(a_hi[i][:, :], raw_a[:, :], ACT.Copy).then_inc(wa_hi_made, 1)

        def head_b(h, i):
            act.wait_ge(raw_b_loaded, 16 * h + 16)
            act.activation(b_hi[i][:, :], raw_b[:, :], ACT.Copy).then_inc(wb_hi_made, 1)

        def move_form(s, base, odd, n):
            act.wait_ge(st_filled, base + n + 1)
            wait(act, form_split, s)
            act.activation(form_f[:, :], st[(odd + n) % 2][:, 0:P], ACT.Copy)
            act.activation(form_hi[:, :], st[(odd + n) % 2][:, 0:P], ACT.Copy).then_inc(st_freed, 1)

        def move_projected(s, i, base, odd, n):
            act.wait_ge(st_filled, base + n + 1)
            wait(act, q_split, s)
            act.activation(q_f[:, :], st[(odd + n) % 2][:, :], ACT.Copy)
            act.activation(q_hi[i][:, :], st[(odd + n) % 2][:, :], ACT.Copy).then_inc(st_freed, 1)

        def move_den(s, half, base, n):
            act.wait_ge(st_filled, base + n + 1)
            wait(act, den_used, 2 * s - 1 + half)
            act.activation(den[:, half * TPH:(half + 1) * TPH], st[(ST_F + n) % 2][:, 0:TPH],
                           ACT.Copy).then_inc(st_freed, 1)

        def move_context(s, half):
            act.wait_ge(prob_used, USED_F + 8 * s + 4 * half + 4)
            wait(act, ctx_split, 2 * s + half)
            act.activation(ctx_f[:, :], pv[:, :], ACT.Copy)
            act.activation(ctx_hi[:, half * HALF:(half + 1) * HALF], pv[:, :], ACT.Copy).then_inc(ctx_hi_made, 1)

        def head_values(s, i, half):
            act.wait_ge(ring_freed, values_freed(s, half))
            ts = slice(half * TPH, (half + 1) * TPH)
            act.activation(v_hi[i][:, ts, :], v_acc[:, ts, :], ACT.Copy).then_inc(v_hi_made, 1)

        def make_diag(s, i, half):
            act.wait_ge(m2_made, 2 * s + half + 1)
            for t in range(half * TPH, (half + 1) * TPH):
                ins = act.activation(diag[i][:, t, :], neg_ident[:, :], ACT.Copy, scale=m2[:, t:t + 1])
            ins.then_inc(diag_made, 1)

        def step(s, r, h, last=False):
            i = r % 2
            base, n = ST_F + PER_ST_F * s, int(first(s))
            if not last:
                move_form(s + 1, base, ST_F, n)
                move_projected(s + 1, 1 - i, base, ST_F, n + 1)
                n += 2
            for beat in range(8):
                if beat == 1 and not first(s):
                    move_den(s - 1, 1, base, n)
                    n += 1
                if beat == 5:
                    move_den(s, 0, base, n)
                    n += 1
                act.wait_ge(prob_used, USED_F + (8 * s + beat - 1 if beat or not first(s) else 0))
                if beat % 4:
                    wait(act, prob_summed, PER_SUM * s + 3 * (beat // 4) + (0, 0, -1, 1)[beat % 4])
                act.wait_ge(st_filled, base + n + 1)
                bank = st[(ST_F + n) % 2]
                act.activation(prob_hi[:, beat % 2, :], bank[:, :], ACT.Exp, scale=SCALE2)
                act.activation(prob[:, prob_at(beat), :], bank[:, :], ACT.Exp, scale=SCALE2).then_inc(st_freed, 1)
                n += 1
                if beat == 0:
                    if not first(s):
                        move_context(s - 1, 1)
                    head_values(s, i, 1)
                    make_diag(s, i, 1)
                if beat == 4:
                    move_context(s, 0)
                    if not last:
                        head_values(s + 1, 1 - i, 0)
                        make_diag(s + 1, 1 - i, 0)
                if beat == 1 and not final(s):
                    (head_b if r % 2 else head_a)(h + 1, (r // 2 + 1) % 2)
            return n

        move_form(0, ST_F - 1, ST_F - 1, 0)
        move_projected(0, 0, ST_F - 1, ST_F - 1, 1)
        act.wait_ge(ring_freed, RING_1)
        head_values(0, 0, 0)
        make_diag(0, 0, 0)
        step(0, 0, 0)
        step(1, 1, 0)
        with act.Fori(0, 3) as it:
            for r in range(2, 6):
                step(4 * it + r, r, 2 * it + r // 2)
        for s in range(14, F_STEPS):
            n = step(s, s % 4, s // 2, last=s == F_STEPS - 1)
        move_context(F_STEPS - 1, 1)
        move_den(F_STEPS - 1, 1, ST_F + PER_ST_F * (F_STEPS - 1), n)

    @block.tensor
    def _(pe):
        pe.wait_ge(consts_made, 1)
        n = 0
        for b in range(B):
            pe.wait_ge(xn_made, b + 1)
            wait(pe, st_freed, n - 1)
            for c in range(NT):
                ins = pe.transpose(st[n % 2][:, c * P:(c + 1) * P], xn[:, b * NT + c, :], ident[:, :])
            ins.then_inc(st_filled, 1)
            n += 1
            if b == 0:
                pe.wait_ge(w_loaded, 16 * 8)
            pe.wait_ge(st_freed, n)
            for t in range(b * NT, (b + 1) * NT, 2):
                pe.wait_ge(st_freed, n - 1)
                for c in range(2):
                    ins = pe.matmul(st[n % 2][:, c * HALF:(c + 1) * HALF], xt[:, (t + c) * P:(t + c + 1) * P], w_in_s[:, :],
                                    start=True, stop=True)
                ins.then_inc(st_filled, 1)
                n += 1

        def product(out, l_hi, l_lo, r_hi, r_lo, begin=True, more=False):
            pe.matmul(out, l_hi, r_hi, start=begin, stop=False)
            pe.matmul(out, l_lo, r_hi, start=False, stop=False)
            return pe.matmul(out, l_hi, r_lo, start=False, stop=not more)

        def form(hp, base, odd, n):
            pe.wait_ge(st_freed, base + n - 1)
            product(st[(odd + n) % 2][:, 0:P], a_hi[hp][:, 0:P], a_lo[hp][:, 0:P], a_hi[hp][:, P:2 * P],
                    a_lo[hp][:, P:2 * P]).then_inc(st_filled, 1)

        def project(s, i, base, odd, n):
            pe.wait_ge(form_split, s + 1)
            pe.wait_ge(st_freed, base + n - 1)
            for half in range(2):
                cols = slice(i * S + half * HALF, i * S + (half + 1) * HALF)
                ins = product(st[(odd + n) % 2][:, half * HALF:(half + 1) * HALF], form_hi[:, :], form_lo[:, :],
                              x_hi[:, cols], x_lo[:, cols])
            ins.then_inc(st_filled, 1)

        def turn_stacks(u, base, odd, n, i):
            pe.wait_ge(stack_made, u + 1)
            for k, buf in enumerate((ks[i], qs[i])):
                wait(pe, st_freed, base + n + k - 1)
                for c in range(NT):
                    ins = pe.transpose(st[(odd + n + k) % 2][:, c * P:(c + 1) * P], buf[:, c, :], ident[:, :])
                ins.then_inc(st_filled, 1)

        def turn_queries(u, base, odd, n, i, half):
            pe.wait_ge(max_made, 2 * u + half + 1)
            pe.wait_ge(st_freed, base + n - 1)
            for c in range(TPH):
                ins = pe.transpose(st[(odd + n) % 2][:, c * P:(c + 1) * P], qs[i][:, half * TPH + c, :], ident[:, :])
            ins.then_inc(st_filled, 1)

        def query_scores(base, odd, n, i, part, q):
            tile, k, j = part // 2, q // 2, 2 * (part % 2) + q % 2
            wait(pe, ring_freed, base + n - 2)
            pe.matmul(ring[(odd + n) % RING][:, :], q_t[i][:, j, tile * P:(tile + 1) * P],
                      k_t[i][:, k * HALF:(k + 1) * HALF], start=True, stop=True).then_inc(ring_filled, 1)
            return n + 1

        def turn_output(t, base, odd, n, half):
            pe.wait_ge(o_t_made, 2 * t + half + 1)
            pe.wait_ge(ring_freed, base + n - 2)
            for c in range(TPH):
                ins = pe.transpose(ring[(odd + n) % RING][:, c * P:(c + 1) * P], o_t[:, half, c * P:(c + 1) * P], ident[:, :])
            ins.then_inc(ring_filled, 1)
            return n + 1

        def att_values(t, i, beat, made):
            half, kt = beat // 8, beat % 8
            if kt == 0:
                wait(pe, o_t_made, 2 * t + half)
                pe.wait_ge(v_stack_made, t + 1)
            pe.wait_ge(st_freed, made)
            for j in range(GROUP):
                ins = pe.matmul(pv[j * SLOT:(j + 1) * SLOT, :], v_st[i][:, kt, j, :],
                                prob[:, 2 * (beat % 2) + j // 2, (j % 2) * HALF:(j % 2 + 1) * HALF],
                                start=kt == 0, stop=kt == NT - 1)
            ins.then_inc(prob_used, 1)

        def att_step(t, i, prep=True):
            sb_, s_n = ST_A + PER_ST_A * t, 0
            rb, r_n = RING_A + PER_RING_A * t, int(first(t))
            if prep:
                turn_stacks(t + 1, sb_, ST_A, s_n, 1 - i)
                s_n += 2
            m = 0
            for beat in range(16):
                half, kt = beat // 8, beat % 8
                if beat == 4:
                    turn_queries(t, sb_, ST_A, s_n, i, 1)
                    s_n += 1
                if beat == 10:
                    r_n = turn_output(t, rb, RING_A, r_n, 0)
                if beat == 11 and prep:
                    turn_queries(t + 1, sb_, ST_A, s_n, 1 - i, 0)
                    s_n += 1
                if beat == 0 and not first(t):
                    att_values(t - 1, 1 - i, 15, sb_)
                if kt == 0:
                    pe.wait_ge(q_spread, 3 * t + (2 if half == 0 else 4 if prep else 3))
                gaps = (1, 2, 3, 5) if beat >= 6 else (0, 1, 2, 3, 5) if beat >= 2 else (3, 4, 5, 5) if beat else ()
                for place in range(6):
                    if place < GROUP:
                        if place % 2 == 0:
                            pe.wait_ge(st_freed, sb_ + s_n - 1)
                        ins = pe.matmul(st[(ST_A + s_n) % 2][:, (place % 2) * HALF:(place % 2 + 1) * HALF],
                                        k_t[i][:, kt * P:(kt + 1) * P], q_t[i][:, place, half * HALF:(half + 1) * HALF],
                                        start=True, stop=True)
                        if place % 2:
                            ins.then_inc(st_filled, 1)
                            s_n += 1
                    elif place == GROUP and beat:
                        att_values(t, i, beat - 1, made)
                    if place == GROUP - 1 and beat == 1 and not first(t):
                        r_n = turn_output(t - 1, rb, RING_A, r_n, 1)
                    if prep and place == GROUP - 1 and beat == 1:
                        pe.wait_ge(heads_spread, (GROUP - 1) * (t + 2))
                        pe.wait_ge(q_spread, 3 * t + 3)
                    for _ in range(gaps.count(place) if prep else 0):
                        r_n = query_scores(rb, RING_A, r_n, 1 - i, m // 4, m % 4)
                        m += 1
                made = sb_ + s_n
            return rb, r_n

        turn_stacks(0, ST_INIT, ST_INIT, 0, 0)
        pe.wait_ge(heads_spread, GROUP - 1)
        pe.wait_ge(q_spread, 1)
        n = 0
        for part in range(16):
            for q in range(4):
                n = query_scores(0, 0, n, 0, part, q)
            if part == 9:
                turn_queries(0, ST_INIT, ST_INIT, 2, 0, 0)
        att_step(0, 0)
        with pe.Fori(0, 3) as it:
            att_step(2 * it + 1, 1)
            att_step(2 * it + 2, 0)
        rb, n = att_step(A_STEPS - 1, 1, prep=False)
        att_values(A_STEPS - 1, 1, 15, ST_F - 1)
        n = rb + turn_output(A_STEPS - 1, rb, rb, n, 1)

        pe.wait_ge(x_lo_made, B)
        pe.wait_ge(wa_split, 1)
        form(0, ST_F - 1, ST_F - 1, 0)

        for q in range(TT // TPH):
            if q == 0:
                pe.wait_ge(ring_freed, RING_AO)
            pe.wait_ge(ring_freed, n - 2)
            for c in range(TPH):
                ins = pe.transpose(ring[n % RING][:, c * P:(c + 1) * P], xn[:, q * TPH + c, :], ident[:, :])
            ins.then_inc(ring_filled, 1)
            n += 1
        project(0, 0, ST_F - 1, ST_F - 1, 1)
        for q in range(TT // TPH):
            pe.wait_ge(ring_freed, RING_AO + q + 1)
            pe.wait_ge(ring_freed, n - 2)
            for c in range(TPH):
                t = q * TPH + c
                ins = pe.matmul(ring[n % RING][:, c * P:(c + 1) * P], xt[:, t * P:(t + 1) * P], wo_s[:, :],
                                start=True, stop=True)
            ins.then_inc(ring_filled, 1)
            n += 1
        assert n == RING_1

        def experts(base, odd, n, l_hi, l_lo, tile, r_hi, r_lo, half):
            rows = slice(tile * P, (tile + 1) * P)
            pe.wait_ge(ring_freed, base + n - 2)
            product(ring[(odd + n) % RING][:, :], l_hi[:, rows], l_lo[:, rows], r_hi[:, half], r_lo[:, half]).then_inc(ring_filled, 1)
            return n + 1

        def values(base, odd, n, i, hp, beat, e):
            half = slice(2 * P + e * HALF, 2 * P + (e + 1) * HALF)
            return experts(base, odd, n, x_hi, x_lo, i * NT + beat, a_hi[hp], a_lo[hp], half)

        def outputs(base, odd, n, hp, beat, e):
            return experts(base, odd, n, ctx_hi, ctx_lo, beat, b_hi[hp], b_lo[hp], slice(e * HALF, (e + 1) * HALF))

        def maxima(base, odd, n, i, tile, k):
            pe.wait_ge(ring_freed, base + n - 2)
            keys = slice(i * S + k * HALF, i * S + (k + 1) * HALF)
            pe.matmul(ring[(odd + n) % RING][:, :], q_hi[i][:, tile * P:(tile + 1) * P], x_hi[:, keys],
                      start=True, stop=True).then_inc(ring_filled, 1)
            return n + 1

        def denominators(s, half, base, odd, n):
            pe.wait_ge(prob_total, 2 * s + half + 1)
            pe.wait_ge(st_freed, base + n - 1)
            for c in range(TPH):
                ins = pe.matmul(st[(odd + n) % 2][:, c:c + 1], p_sum[:, half, c * P:(c + 1) * P], ones[:, 0:1],
                                start=True, stop=True)
            ins.then_inc(st_filled, 1)
            return n + 1

        def att_products(s, i, beat):
            half, n = beat // 4, beat % 4
            if n == 0:
                if first(s) and half == 0:
                    pe.wait_ge(o_t_made, 2 * A_STEPS)
                else:
                    pe.wait_ge(ctx_hi_made, 2 * s + half)
            if half == 0 and n % 2 == 0:
                pe.wait_ge(v_split, 2 * s + n // 2 + 1)
            pe.wait_ge(prob_split, 8 * s + beat + 1)
            for k in range(2):
                kt, cols = 2 * n + k, slice(k * HALF, (k + 1) * HALF)
                ins = product(pv[:, :], v_hi[i][:, kt, :], v_lo[i][:, kt, :], prob_hi[:, beat % 2, cols],
                              prob_lo[:, beat % 2, cols], begin=kt == 0, more=kt < NT - 1)
            ins.then_inc(prob_used, 1)

        def output_pair(base, n, tile):
            pe.wait_ge(ctx_split, 2 * (F_STEPS - 1) + tile // TPH + 1)
            for e in range(2):
                for t in (tile, tile + 1):
                    n = outputs(base, RING_F, n, (H2 - 1) % 2, t, e)
            return n

        def step(s, r, h, prep=True):
            i, post = r % 2, not first(s)
            nh, ph = (r + 1) // 2 % 2, (r - 1) // 2 % 2
            sb_, s_n = ST_F + PER_ST_F * s, int(first(s))
            rb, r_n = RING_F + PER_RING_F * s, 16 * int(first(s))
            if prep:
                if i:
                    pe.wait_ge(wa_split, h + 2)
                form(nh, sb_, ST_F, s_n)
                s_n += 2
            for beat in range(8):
                half, n = beat // 4, beat % 4
                if beat == 1 and post:
                    s_n = denominators(s - 1, 1, sb_, ST_F, s_n)
                if beat == 5:
                    s_n = denominators(s, 0, sb_, ST_F, s_n)
                if post and n == 0:
                    if i == 1 and half == 0:
                        pe.wait_ge(wb_split, h + 1)
                    pe.wait_ge(ctx_split, 2 * s - 1 + half)
                if prep:
                    r_n = values(rb, RING_F, r_n, 1 - i, nh, beat, 0)
                if post:
                    r_n = outputs(rb, RING_F, r_n, ph, beat, 0)
                if prep:
                    r_n = values(rb, RING_F, r_n, 1 - i, nh, beat, 1)
                    if beat == 0:
                        project(s + 1, 1 - i, sb_, ST_F, s_n - 1)
                if beat == 0:
                    pe.wait_ge(q_split, s + 1)
                if n == 0:
                    pe.wait_ge(diag_made, 2 * s + half + 1)
                pe.wait_ge(st_freed, sb_ + s_n - 1)
                cols = slice(half * HALF, (half + 1) * HALF)
                for k in range(2):
                    keys = slice(i * S + (2 * n + k) * P, i * S + (2 * n + k + 1) * P)
                    out = st[(ST_F + s_n) % 2][:, k * HALF:(k + 1) * HALF]
                    product(out, x_hi[:, keys], x_lo[:, keys], q_hi[i][:, cols], q_lo[i][:, cols], more=True)
                    ins = pe.matmul(out, ones_r[:, :], diag[i][:, half * TPH:(half + 1) * TPH, :], start=False, stop=True)
                    if k == 0 and post:
                        r_n = outputs(rb, RING_F, r_n, ph, beat, 1)
                ins.then_inc(st_filled, 1)
                s_n += 1
                if prep:
                    if beat == 0:
                        pe.wait_ge(st_freed, moved_fill(s + 1, 1) + 1)
                    r_n = maxima(rb, RING_F, r_n, 1 - i, beat, 0)
                if beat:
                    att_products(s, i, beat - 1)
                elif post:
                    att_products(s - 1, 1 - i, 7)
                if prep:
                    r_n = maxima(rb, RING_F, r_n, 1 - i, beat, 1)
                elif beat > 5:
                    r_n = output_pair(rb, r_n, 2 * (beat - 6))
            return sb_, s_n, rb, r_n

        pe.wait_ge(st_freed, moved_fill(0, 1) + 1)
        n = 0
        for beat in range(0, 8, 2):
            for e in range(2):
                for tile in (beat, beat + 1):
                    n = values(RING_1, RING_1, n, 0, 0, tile, e)
            for tile in (beat, beat + 1):
                for k in range(2):
                    n = maxima(RING_1, RING_1, n, 0, tile, k)
        step(0, 0, 0)
        step(1, 1, 0)
        with pe.Fori(0, 3) as it:
            for r in range(2, 6):
                step(4 * it + r, r, 2 * it + r // 2)
        for s in range(14, F_STEPS):
            sb_, s_n, rb, r_n = step(s, s % 4, s // 2, prep=s < F_STEPS - 1)
        att_products(F_STEPS - 1, (F_STEPS - 1) % 2, 7)
        denominators(F_STEPS - 1, 1, sb_, ST_F, s_n)
        for tile in (4, 6):
            r_n = output_pair(rb, r_n, tile)

    @block.vector
    def _(dve):
        chain = [0, 0]

        def mark(ins):
            chain[1] += 1
            return ins.then_inc(dve_step, 1)

        def settle(but=0):
            dve.wait_ge(dve_step, chain[0] + chain[1] - but)

        def then(ins):
            mark(ins)
            settle()

        for b in range(B):
            dve.wait_ge(x_loaded[b], 16)
            ts = slice(b * NT, (b + 1) * NT)
            for t in range(b * NT, (b + 1) * NT):
                ins = dve.bn_stats(stats[:, t, :], acc[:, t, :])
            mark(ins)
            settle()
            for t in range(b * NT, (b + 1) * NT):
                ins = dve.bn_aggr(mv[:, t, :], stats[:, t, :])
            mark(ins)
            settle()
            var = mv[:, ts, 1:2].rearrange("p t a -> p (t a)")
            dve.tensor_scalar(var, var, EPS, None, ALU.add).then_inc(var_made, 1)
            dve.wait_ge(sqrt_made, b + 1)
            r, z = rstd[:, ts], newton[:, ts]
            then(dve.reciprocal(r, r))
            then(dve.tensor_tensor(z, r, r, ALU.mult))
            then(dve.tensor_tensor(z, z, var, ALU.mult))
            then(dve.tensor_scalar(z, z, -0.5, 1.5, ALU.mult, ALU.add))
            then(dve.tensor_tensor(r, r, z, ALU.mult))
            for t in range(b * NT, (b + 1) * NT):
                ins = dve.tensor_scalar(xn[:, t, :], acc[:, t, :], mv[:, t, 0:1], rstd[:, t:t + 1], ALU.subtract, ALU.mult)
            ins.then_inc(xn_made, 1)
        dve.wait_ge(consts_made, 1)
        dve.tensor_reduce(head_mask[:, :], ident[:, :].rearrange("p (j r) -> p j r", r=SLOT), AX_X,
                          ALU.max).then_inc(mask_made, 1)
        dve.wait_ge(w_loaded, 16 * 8)
        for b in range(B):
            ts = slice(b * NT, (b + 1) * NT)
            dve.wait_ge(st_freed, PER_ST_INIT * (b + 1))
            bias = b_in_s[:, 0:2 * P].rearrange("p (a n) -> p a n", a=1).broadcast_to([P, NT, 2 * P])
            then(dve.tensor_tensor(qk_tok[:, ts, :], qk_tok[:, ts, :], bias, ALU.add))
            for k in range(2):
                v = qk_tok[:, ts, k * P:(k + 1) * P].rearrange("p t (h e) -> p t h e", e=HD1)
                a = t_a[:, k * S:(k + 1) * S].rearrange("p (t h e) -> p t h e", h=NH1, e=HD1)
                c = t_b[:, k * S:(k + 1) * S].rearrange("p (t h e) -> p t h e", h=NH1, e=HD1)
                hf = HD1 // 2

                def table(tab, lo, hi):
                    return tab[:, :, lo:hi].rearrange("p t (a e) -> p t a e", a=1).broadcast_to([P, NT, NH1, hi - lo])

                dve.tensor_tensor(a, v, table(cos_s, 0, HD1), ALU.mult)
                dve.tensor_tensor(c[:, :, :, 0:hf], v[:, :, :, hf:HD1], table(sin_s, 0, hf), ALU.mult)
                mark(dve.tensor_tensor(c[:, :, :, hf:HD1], v[:, :, :, 0:hf], table(sin_s, hf, HD1), ALU.mult))
                settle()
                ins = dve.tensor_tensor(v, a, c, ALU.add)
            ins.then_inc(tok_made, 1)

        cells = TT * 2 * H2

        def cube(a):
            return a.rearrange("p (c e) -> p c e", e=E2)

        def wide(a):
            return a.broadcast_to([P, cells, E2])

        neg = gates[:, :, :].rearrange("p t (c e) -> p (t c) e", e=E2)
        oh1, eq = cube(t_a[:, :]), cube(t_b[:, :])
        oh2 = cube(qk_tok[:, 0:NT, :].rearrange("p t n -> p (t n)"))
        top = [small[:, k, :].rearrange("p (c a) -> p c a", a=1) for k in range(5)]
        rank_w = rank_s[:, :].rearrange("p (a e) -> p a e", a=1).broadcast_to([P, cells, E2])

        def begin_gates(k):
            if k == 0:
                dve.wait_ge(neg_made, 1)
                mark(dve.tensor_reduce(top[0], neg, AX_X, ALU.max))
            else:
                settle()
                mark(dve.tensor_tensor(oh1, neg, wide(top[0]), ALU.is_equal))

        def end_gates():
            dve.wait_ge(stack_made, A_STEPS)
            settle()
            for k, oh in enumerate((oh1, oh2)):
                if k:
                    then(dve.tensor_reduce(top[1], eq, AX_X, ALU.max))
                    then(dve.tensor_tensor(oh2, eq, wide(top[1]), ALU.is_equal))
                then(dve.tensor_tensor(oh, oh, rank_w, ALU.mult))
                then(dve.tensor_reduce(top[2], oh, AX_X, ALU.max))
                then(dve.tensor_tensor(oh, oh, wide(top[2]), ALU.is_equal))
                if k == 0:
                    then(dve.scalar_tensor_tensor(out=eq, in0=oh1, scalar=-3e38, in1=neg, op0=ALU.mult, op1=ALU.add))
            for k in range(2):
                then(dve.reciprocal(top[k], top[k]))
            then(dve.tensor_tensor(top[3], top[0], top[1], ALU.add))
            then(dve.tensor_scalar(top[3], top[3], -1e-9, None, ALU.min))
            then(dve.reciprocal(top[4], top[3]))
            then(dve.tensor_scalar(top[4], top[4], rs_b[:, 0:1], None, ALU.mult))
            dve.tensor_tensor(top[0], top[0], top[4], ALU.mult).then_inc(weights_made, 1)
            then(dve.tensor_tensor(top[1], top[1], top[4], ALU.mult))
            then(dve.tensor_tensor(oh2, oh2, wide(top[1]), ALU.mult))
            dve.wait_ge(gates_made, 1)
            then(dve.tensor_tensor(neg, oh1, oh2, ALU.add))

        def maxima(base, odd, n, i, part):
            tile = part // 2
            for k in range(2):
                for j in range(2 * (part % 2), 2 * (part % 2) + 2):
                    dve.wait_ge(ring_filled, base + n + 1)
                    ins = dve.tensor_reduce(mx1[i][:, tile, j, k:k + 1], ring[(odd + n) % RING][:, :], AX_X,
                                            ALU.max).then_inc(ring_freed, 1)
                    n += 1
            if part % 8 == 7:
                dve.wait_ge(ring_freed, base + n)
                ts = slice(part // 8 * TPH, (part // 8 + 1) * TPH)
                q = qs[i][:, ts, :].rearrange("p t (j r) -> p t j r", r=SLOT)[:, :, :, ROWS:ROWS + 1]
                dve.tensor_tensor(q.bitcast(F32R), mx1[i][:, ts, :, 0:1], mx1[i][:, ts, :, 1:2], ALU.max).then_inc(max_made, 1)
            return n

        def spread_heads(t, i):
            dve.wait_ge(st_freed, stack_fill(t) + 1)
            for j in range(GROUP - 1):
                dve.tensor_scalar(q_t[i][:, j, :], q_turned[:, 0:S], head_mask[:, j:j + 1], None, ALU.mult).then_inc(heads_spread, 1)

        def divide(t, g, i, base, odd, n, half):
            dve.wait_ge(ring_filled, base + n + 1)
            v = ring[(odd + n) % RING][:, :].rearrange("p (t j r) -> p t j r", j=GROUP, r=SLOT)
            d = rden1[:, half, :, :].rearrange("p t (j a) -> p t j a", a=1)
            mark(dve.reciprocal(d, v[:, :, :, HD1:HD1 + 1]))
            settle()
            out = xn[:, i * NT + half * TPH:i * NT + (half + 1) * TPH, bass.ds(g * (GROUP * HD1), GROUP * HD1)]
            ins = dve.tensor_tensor(out.rearrange("p t (j e) -> p t j e", e=HD1), v[:, :, :, 0:HD1],
                                    d.broadcast_to([P, TPH, GROUP, HD1]), ALU.mult)
            ins.then_inc(ring_freed, 1)
            return ins, n + 1

        def att_step(t, g, gp, i):
            base, n = RING_A + PER_RING_A * t, int(first(t))
            spread_heads(t + 1, 1 - i)
            if not first(t):
                _, n = divide(t - 1, gp, 1 - i, base, RING_A, n, 1)
            for part in range(16):
                if part == 10:
                    _, n = divide(t, g, i, base, RING_A, n, 0)
                n = maxima(base, RING_A, n, 1 - i, part)
                if first(t) and part in (7, 12):
                    begin_gates(int(part == 12))
            return base, n

        spread_heads(0, 0)
        n = 0
        for part in range(16):
            n = maxima(0, 0, n, 0, part)
        att_step(0, 0, 0, 0)
        chain[:] = [chain[0] + chain[1], 0]
        start, per = chain[0], 2 * 2
        with dve.Fori(0, 3) as it:
            chain[0] = start + per * it
            att_step(2 * it + 1, it, it, 1)
            att_step(2 * it + 2, it + 1, it, 0)
        assert chain[1] == per
        chain[:] = [start + 3 * per, 0]
        last, n = A_STEPS - 1, 0
        base = RING_A + PER_RING_A * last
        _, n = divide(last - 1, NG - 1, 0, base, base, n, 1)
        end_gates()
        for half in range(2):
            _, n = divide(last, NG - 1, 1, base, base, n, half)
        n += base

        def split_form(s):
            dve.wait_ge(st_freed, moved_fill(s, 0) + 1)
            dve.tensor_tensor(form_lo[:, :], form_f[:, :], form_hi[:, :], ALU.subtract).then_inc(form_split, 1)

        split_form(0)
        for q in range(TT // TPH):
            dve.wait_ge(ring_filled, n + 1)
            dve.tensor_copy(xt[:, q * HALF:(q + 1) * HALF], ring[n % RING][:, :]).then_inc(ring_freed, 1)
            n += 1

        for q in range(TT // TPH):
            dve.wait_ge(ring_filled, n + 1)
            dve.wait_ge(bias_added, 1)
            part = acc[:, q * TPH:(q + 1) * TPH, :]
            ins = dve.tensor_tensor(part, ring[n % RING][:, :].rearrange("p (t d) -> p t d", d=D), part, ALU.add)
            ins.then_inc(ring_freed, 1)
            n += 1

        def head_gates(h, off, i):
            a = gates[:, i * NT:(i + 1) * NT, bass.ds(h * E2 + off, E2)]
            return a

        def value_gates(h, i):
            mark(dve.tensor_copy(gv[:, :, :], head_gates(h, 0, i)))
            settle()

        def output_gates(s, h, i, half):
            ts = slice(half * TPH, (half + 1) * TPH)
            dve.wait_ge(st_freed, den_fill(s, half) + 1)
            dve.reciprocal(rden[:, ts], den[:, ts]).then_inc(den_used, 1)
            dve.wait_ge(den_used, 2 * s + half + 1)
            g = head_gates(h, H2 * E2, i)[:, ts, :]
            r = rden[:, ts].rearrange("p (t a) -> p t a", a=1)
            mark(dve.tensor_tensor(go[:, ts, :], g, r.broadcast_to([P, TPH, E2]), ALU.mult))
            settle()

        def experts(base, odd, n, beat, i, made, prep, post):
            both = int(prep and post)
            if prep and beat % 4 == 0:
                wait(dve, v_split, 2 * made + beat // 4 - 1)
            if post:
                dve.wait_ge(ring_freed, base + n - 2)
            both_turns = ((0, 0), (0, 1), (1, 0), (0, 2), (1, 1), (0, 3), (1, 2), (1, 3))
            for e in range(2):
                marks, last = 0, [0, 0]
                for turn, k in (both_turns if both else [(int(post), k) for k in range(4)]):
                    x, at = 4 * e + k, n + turn * both
                    if turn:
                        out, g = acc[:, (1 - i) * NT + beat, :], go[:, beat, x:x + 1]
                    else:
                        out, g = v_acc[:, beat, :], gv[:, beat, x:x + 1]
                    if k == 0:
                        dve.wait_ge(ring_filled, base + at + 1)
                        if e:
                            dve.wait_ge(ring_freed, base + at - both)
                    else:
                        settle(but=marks - last[turn])
                    src = ring[(odd + at) % RING][:, k * P:(k + 1) * P]
                    if x == 0 and turn == 0:
                        ins = dve.tensor_scalar(out, src, g, None, ALU.mult)
                    else:
                        ins = dve.scalar_tensor_tensor(out=out, in0=src, scalar=g, in1=out, op0=ALU.mult, op1=ALU.add)
                    if k < 3:
                        mark(ins)
                        marks += 1
                        last[turn] = marks
                    else:
                        ins.then_inc(ring_freed, 1)
                n += 1 + both
            return n

        def expert_pair(base, odd, n, tiles, out, g, begin):
            if not begin:
                dve.wait_ge(ring_freed, base + n - 2)
            for e in range(2):
                for k in range(4):
                    for side in range(2):
                        at, x = n + side, 4 * e + k
                        if k == 0:
                            dve.wait_ge(ring_filled, base + at + 1)
                            if e:
                                dve.wait_ge(ring_freed, base + at - 1)
                        else:
                            settle(but=int(k < 3 or side == 0))
                        src, to = ring[(odd + at) % RING][:, k * P:(k + 1) * P], out[:, tiles[side], :]
                        gate = g[:, tiles[side] % NT, x:x + 1]
                        if x == 0 and begin:
                            ins = dve.tensor_scalar(to, src, gate, None, ALU.mult)
                        else:
                            ins = dve.scalar_tensor_tensor(out=to, in0=src, scalar=gate, in1=to, op0=ALU.mult, op1=ALU.add)
                        if k < 3:
                            mark(ins)
                        else:
                            ins.then_inc(ring_freed, 1)
                n += 2
            return n

        def query_maxima(base, odd, n, made, tile):
            for k in range(2):
                dve.wait_ge(ring_filled, base + n + 1)
                ins = dve.tensor_reduce(mx2[:, tile, k:k + 1], ring[(odd + n) % RING][:, :], AX_X, ALU.max).then_inc(ring_freed, 1)
                n += 1
            if tile % TPH == TPH - 1:
                dve.wait_ge(ring_freed, base + n)
                half = tile // TPH
                wait(dve, diag_made, 2 * made + half - 1)
                ts = slice(half * TPH, (half + 1) * TPH)
                m = m2[:, ts].rearrange("p (t a) -> p t a", a=1)
                dve.tensor_tensor(m, mx2[:, ts, 0:1], mx2[:, ts, 1:2], ALU.max).then_inc(m2_made, 1)
            return n

        def step(s, r, h, h_next, h_last, prep=True):
            i, post = r % 2, not first(s)
            base, n = RING_F + PER_RING_F * s, 16 * int(first(s))
            if prep:
                split_form(s + 1)
                value_gates(h_next, 1 - i)
            for beat in range(8):
                n = experts(base, RING_F, n, beat, i, s + 1, prep, post)
                if beat == 2 and post:
                    output_gates(s - 1, h_last, 1 - i, 1)
                if beat == 6:
                    output_gates(s, h, i, 0)
                if beat > 5 and not prep:
                    tile = NT + 2 * (beat - 6)
                    n = expert_pair(base, RING_F, n, (tile, tile + 1), acc, go, False)
                if prep:
                    n = query_maxima(base, RING_F, n, s + 1, beat)
            return base, n

        value_gates(0, 0)
        n = 0
        for beat in range(0, 8, 2):
            n = expert_pair(RING_1, RING_1, n, (beat, beat + 1), v_acc, gv, True)
            for tile in (beat, beat + 1):
                n = query_maxima(RING_1, RING_1, n, 0, tile)
        step(0, 0, 0, 0, None)
        step(1, 1, 0, 1, 0)
        chain[:] = [chain[0] + chain[1], 0]
        start, per = chain[0], 4 * (1 + 8 * 12 + 2)
        with dve.Fori(0, 3) as it:
            chain[0] = start + per * it
            for r in range(2, 6):
                step(4 * it + r, r, 2 * it + r // 2, 2 * it + (r + 1) // 2, 2 * it + (r - 1) // 2)
        assert chain[1] == per, (chain, per)
        chain[:] = [start + 3 * per, 0]
        for s in range(14, F_STEPS):
            base, n = step(s, s % 4, s // 2, (s + 1) // 2, (s - 1) // 2, prep=s < F_STEPS - 1)
        last = F_STEPS - 1
        output_gates(last, H2 - 1, 1, 1)
        for tile in (NT + 4, NT + 6):
            n = expert_pair(base, RING_F, n, (tile, tile + 1), acc, go, False)

    ctx.close()


def kernel(L0_attn_x, L0_attn_wq, L0_attn_bq, L0_attn_wk, L0_attn_bk, L0_attn_wv, L0_attn_bv, L0_attn_wo, L0_attn_bo,
           L0_ffn_q_w, L0_ffn_k_w, L0_ffn_v_w, L0_ffn_o_w, L0_ffn_sel_v_w, L0_ffn_sel_o_w, L0_ffn_route_scale):
    import numpy as np
    import concourse.bacc as bacc
    from concourse.bass_utils import run_bass_kernel_spmd

    inv = (np.float32(1.0) / np.float32(10000.0) ** (np.arange(0, HD1, 2, dtype=np.float32) / np.float32(HD1))).astype(np.float32)
    ang = np.arange(S, dtype=np.float32)[:, None] * inv[None, :]
    cos = np.concatenate([np.cos(ang), np.cos(ang)], 1).astype(np.float32)
    sin = np.concatenate([-np.sin(ang), np.sin(ang)], 1).astype(np.float32)
    rank = np.arange(E2, 0, -1).astype(np.float32)
    f = np.asarray
    q_w = f(L0_ffn_q_w).reshape(H2, P, D)
    k_w = f(L0_ffn_k_w).reshape(H2, P, D)
    v_w = f(L0_ffn_v_w).reshape(H2, E2, D, P).transpose(0, 2, 1, 3).reshape(H2, D, E2 * P)
    o_w = f(L0_ffn_o_w).reshape(H2, E2, P, D).transpose(0, 2, 1, 3).reshape(H2, P, E2 * D)
    arrays = {
        "x": f(L0_attn_x),
        "w_in": np.concatenate([f(L0_attn_wq).T, f(L0_attn_wk).T, f(L0_attn_wv).T, f(L0_ffn_sel_v_w).T, f(L0_ffn_sel_o_w).T], 1),
        "wo_t": f(L0_attn_wo).T,
        "b_in": np.concatenate([f(L0_attn_bq), f(L0_attn_bk), f(L0_attn_bv)]),
        "bo": f(L0_attn_bo),
        "rs": f(L0_ffn_route_scale),
        "cos": cos, "sin": sin, "rank": rank,
        "wf": np.concatenate([q_w, k_w, v_w, o_w], 2),
    }
    nc = bacc.Bacc("TRN2", target_bir_lowering=False, num_devices=1)
    feed, args = {}, {}
    for name, a in arrays.items():
        feed[f"in_{name}"] = np.ascontiguousarray(a)
        args[name] = nc.dram_tensor(f"in_{name}", a.shape, F32, kind="ExternalInput").ap()
    args["out"] = nc.dram_tensor("out", (B, S, D), F32, kind="ExternalOutput").ap()
    build(nc, **args)
    return run_bass_kernel_spmd(nc, [feed], core_ids=[0]).results[0]["out"]
```
